# Optimizing a Trainium2 kernel written in Bass

```python
import numpy as np
import jax
import jax.numpy as jnp

def _softmax(x, axis=-1):
    return jax.nn.softmax(x, axis=axis)

def _gelu(x):
    return jax.nn.gelu(x, approximate=True)

def _silu(x):
    return jax.nn.silu(x)

def _sigmoid(x):
    return jax.nn.sigmoid(x)

def _layernorm(x, axis=-1, eps=1e-05):
    m = jnp.mean(x, axis=axis, keepdims=True)
    v = jnp.var(x, axis=axis, keepdims=True)
    return (x - m) / jnp.sqrt(v + eps)

def _scatter_add(tgt, idx, src, axis=0):
    return tgt.at[idx].add(src)

def _segment_sum(src, seg, n):
    return jax.ops.segment_sum(src, seg, n)
kernel_name = 'mk_gnn_preln_d2_gnn_r32_f59db1'

def setup_inputs(seed: int=0):
    np.random.seed(seed)
    _w = jnp.asarray

    def _rec_inputs():
        import jax
        import jax.numpy as jnp
        _gk = jax.random.key(seed)
        x = -0.0001006 + 1 * jax.random.normal(jax.random.fold_in(_gk, 1), (3125, 48), jnp.float32)
        _s = jax.random.randint(jax.random.fold_in(_gk, 2), (50000,), 0, 3125, jnp.int32)
        _d = jax.random.randint(jax.random.fold_in(_gk, 3), (50000,), 0, 3125, jnp.int32)
        _loop = jnp.arange(3125, dtype=jnp.int32)
        src = jnp.concatenate([_s, _d, _loop])
        dst = jnp.concatenate([_d, _s, _loop])
        _o = jnp.argsort(dst, stable=True)
        src = src[_o]
        dst = dst[_o]
        edge_attr_48 = -4.21973e-05 + 0.999841 * jax.random.normal(jax.random.fold_in(_gk, 12), (103125, 48), jnp.float32)
        return (x, src, dst, edge_attr_48)
    x, src, dst, edge_attr_48 = _rec_inputs()

    def _L0_gnn_setup():
        import jax, jax.numpy as jnp
        import numpy as np
        N_NODES = 3125
        N_EDGES = 50000
        D_FEAT = 48
        key = jax.random.key(seed)
        k1, k2, k3, k4 = jax.random.split(key, 4)
        node_feat = jax.random.normal(k1, (N_NODES, D_FEAT), dtype=jnp.float32)
        edge_feat = jax.random.normal(k2, (N_EDGES, D_FEAT), dtype=jnp.float32)
        src = jax.random.randint(k3, (N_EDGES,), 0, N_NODES, dtype=jnp.int32)
        dst = jax.random.randint(k4, (N_EDGES,), 0, N_NODES, dtype=jnp.int32)
        eps = jnp.zeros((1,), dtype=jnp.float32)
        return {'node_feat': node_feat, 'edge_feat': edge_feat, 'src': src, 'dst': dst, 'eps': eps}
    _L0_gnn_all = _L0_gnn_setup()
    _L0_gnn_in = {k: v for k, v in _L0_gnn_all.items() if k in ('eps',)}
    del _L0_gnn_all

    def _L1_gnn_setup():
        import jax, jax.numpy as jnp
        import numpy as np
        N_NODES = 3125
        N_EDGES = 50000
        IN_FEAT = 48
        OUT_FEAT = 48
        key = jax.random.key(seed)
        k_h, k_src, k_dst, k_tw, k_tb, k_pw, k_pb = jax.random.split(key, 7)
        lim = 1.0 / np.sqrt(IN_FEAT)
        return {'h': jax.random.normal(k_h, (N_NODES, IN_FEAT), dtype=jnp.float32), 'theta_w': jax.random.uniform(k_tw, (OUT_FEAT, IN_FEAT), jnp.float32, -lim, lim), 'theta_b': jax.random.uniform(k_tb, (OUT_FEAT,), jnp.float32, -lim, lim), 'phi_w': jax.random.uniform(k_pw, (OUT_FEAT, IN_FEAT), jnp.float32, -lim, lim), 'phi_b': jax.random.uniform(k_pb, (OUT_FEAT,), jnp.float32, -lim, lim), 'src': jax.random.randint(k_src, (N_EDGES,), 0, N_NODES, dtype=jnp.int64), 'dst': jax.random.randint(k_dst, (N_EDGES,), 0, N_NODES, dtype=jnp.int64)}
    _L1_gnn_all = _L1_gnn_setup()
    _L1_gnn_in = {k: v for k, v in _L1_gnn_all.items() if k in ('theta_w', 'theta_b', 'phi_w', 'phi_b')}
    del _L1_gnn_all
    return {'x': x, 'src': src, 'dst': dst, 'edge_attr_48': edge_attr_48, 'L0_gnn_eps': _L0_gnn_in['eps'], 'L1_gnn_theta_w': _L1_gnn_in['theta_w'], 'L1_gnn_theta_b': _L1_gnn_in['theta_b'], 'L1_gnn_phi_w': _L1_gnn_in['phi_w'], 'L1_gnn_phi_b': _L1_gnn_in['phi_b']}

def reference(x, src, dst, edge_attr_48, L0_gnn_eps, L1_gnn_theta_w, L1_gnn_theta_b, L1_gnn_phi_w, L1_gnn_phi_b):
    import jax
    import jax.numpy as jnp

    def _L0_gnn_ref(node_feat, edge_feat, src, dst, eps):
        import jax, jax.numpy as jnp
        import numpy as np
        N_NODES = 3125
        N_EDGES = 50000
        D_FEAT = 48
        m = jax.nn.relu(node_feat[src] + edge_feat)
        neigh = jax.ops.segment_sum(m, dst, num_segments=N_NODES)
        return (1.0 + eps[0]) * node_feat + neigh

    def _L1_gnn_ref(h, theta_w, theta_b, phi_w, phi_b, src, dst):
        import jax, jax.numpy as jnp
        import numpy as np
        N_NODES = 3125
        N_EDGES = 50000
        IN_FEAT = 48
        OUT_FEAT = 48
        phi_all = h @ phi_w.T + phi_b
        diff = h[dst] - h[src]
        e = diff @ theta_w.T + theta_b + phi_all[src]
        out = jax.ops.segment_max(e, dst, num_segments=N_NODES)
        out = jnp.where(jnp.isneginf(out), 0.0, out)
        return out
    h = jnp.maximum(_layernorm(x, axis=-1), 0.0)
    x = x + _L0_gnn_ref(h, edge_attr_48, src, dst, L0_gnn_eps)
    h = jnp.maximum(_layernorm(x, axis=-1), 0.0)
    x = x + _L1_gnn_ref(h, L1_gnn_theta_w, L1_gnn_theta_b, L1_gnn_phi_w, L1_gnn_phi_b, src, dst)
    return x

_drawn_inputs = setup_inputs


def setup_inputs(seed=0):
    import zlib

    import numpy as np

    out = dict(_drawn_inputs(seed))
    spreads = {}
    factors = {'L1_gnn_theta_w': 3.64, 'L1_gnn_theta_b': 8.0, 'L1_gnn_phi_w': 4.336, 'L1_gnn_phi_b': 8.0}
    for name, (base, spread) in spreads.items():
        noise = np.random.default_rng([zlib.crc32(name.encode()), seed]).standard_normal(out[name].shape)
        drawn = base * np.exp(spread * noise) if base else spread * noise
        out[name] = jnp.asarray(drawn.astype(out[name].dtype))
    for name, factor in factors.items():
        out[name] = (out[name] * factor).astype(out[name].dtype)
    return out
```

```python
from contextlib import ExitStack

import concourse.bass as bass
from concourse import mybir

P = 128
ALU = mybir.AluOpType
ACT = mybir.ActivationFunctionType
F32 = mybir.dt.float32
BF16 = mybir.dt.bfloat16
I32 = mybir.dt.int32
AX_X = mybir.AxisListType.X
BIG = 3.0e38
LN_EPS = 1e-5
DVE, POOL, PE, SP, ACTE = (
    mybir.EngineType.DVE,
    mybir.EngineType.Pool,
    mybir.EngineType.PE,
    mybir.EngineType.SP,
    mybir.EngineType.Activation,
)


def gnn_two_layer_kernel(nc, x, src, dst, edge_attr, eps, theta_t, theta_b, phi_t, phi_b, out):
    N, D = x.shape
    E = src.shape[0]
    COLS = -(-E // P)
    LAST = E - (P - 1) * COLS
    T = 31
    CHUNKS = COLS // T
    PAIRS = CHUNKS // 2
    A = -(-N // P)
    NT = N - (A - 1) * P
    FULL = (LAST // T) // 2
    assert COLS == CHUNKS * T and CHUNKS == 2 * PAIRS and FULL == PAIRS - 1 and 0 < LAST < COLS
    PB = 10
    TBL = 5

    table_d = [nc.dram_tensor(f"table{L}_d", (A * P, D), F32) for L in range(2)]
    scan_d = [nc.dram_tensor(f"scan{L}_d", (P * COLS, D), F32) for L in range(2)]

    with ExitStack() as ctx:
        def sb(name, shape, dt=F32):
            return ctx.enter_context(nc.sbuf_tensor(name, shape, dt))

        def psum(name, shape):
            return ctx.enter_context(nc.psum_tensor(name, shape, F32))

        def sem(name):
            return ctx.enter_context(nc.semaphore(name))

        dst_i = sb("dst_i", [P, COLS], I32)
        src_i = sb("src_i", [P, COLS], I32)
        same = sb("same", [P, COLS])
        penalty = sb("penalty", [P, COLS])
        dst_lo = sb("dst_lo", [P, COLS], BF16)
        dst_hi = sb("dst_hi", [P, COLS], BF16)
        idx = [sb(f"idx{s}", [P, T], I32) for s in range(2)]
        gat = [sb(f"gat{s}", [P, T, D]) for s in range(2)]
        attr = [sb(f"attr{s}", [P, T, D]) for s in range(2)]
        msg = [sb(f"msg{s}", [P, D, T + 1]) for s in range(2)]
        keep = [sb(f"keep{s}", [P, D, T + 1]) for s in range(2)]
        state = [sb(f"state{s}", [P, D, T + 1]) for s in range(2)]
        rows = [sb(f"rows{s}", [P, T, D]) for s in range(2)]
        oh_lo = sb("oh_lo", [P, T, P], BF16)
        oh_hi = sb("oh_hi", [P, T, A], BF16)
        xin = sb("xin", [P, A, D])
        cen = sb("cen", [P, A, D])
        hid = sb("hid", [P, A, D])
        val = sb("val", [P, A, D])
        atab = sb("atab", [P, A, D])
        nstat = sb("nstat", [P, 4, A])
        hT = sb("hT", [65, A * P])
        wcat = sb("wcat", [65, 2 * D])
        eps_t = sb("eps_t", [P, 1])
        iota_i = sb("iota_i", [P, P], I32)
        iota_n = sb("iota_n", [P, A * P], I32)
        fixsel = sb("fixsel", [P, A * P])
        iota_f = sb("iota_f", [P, P])
        iota_b = sb("iota_b", [P, P], BF16)
        pidx_i = sb("pidx_i", [P, 1], I32)
        pidx = sb("pidx", [P, 1])
        ident = sb("ident", [P, P])
        tri = sb("tri", [P, P])
        ones = sb("ones", [P, P])
        hist = sb("hist", [P, A])
        cum = sb("cum", [P, 3, A])
        has = sb("has", [P, A])
        end_i = sb("end_i", [P, A], I32)
        edge_i = sb("edge_i", [P, 4], I32)
        edge = sb("edge", [P, 4])
        flag = sb("flag", [P, 8])
        through = [sb(f"through{L}", [P, D]) for L in range(2)]
        throughT = [sb(f"throughT{L}", [D, P]) for L in range(2)]
        trail = sb("trail", [P, D])
        trailT = sb("trailT", [D, P])
        carryT = sb("carryT", [D, P + 1])
        carry = sb("carry", [P, D + 1])
        fixpen = sb("fixpen", [P, A])

        ps_hist = psum("ps_hist", [P, 512])
        ps_small = psum("ps_small", [P, 512])
        ps_fix = psum("ps_fix", [P, 3, 512])
        ps_tab = psum("ps_tab", [P, 2, 512])

        edges_in = sem("edges_in")
        x_in = sem("x_in")
        small_in = sem("small_in")
        w_in = sem("w_in")
        attr_in = [sem(f"attr_in{s}") for s in range(2)]
        table_out = [sem(f"table_out{L}") for L in range(2)]
        gathered = [[sem(f"gathered{L}{s}") for s in range(2)] for L in range(2)]
        stored = [[sem(f"stored{L}{s}") for s in range(2)] for L in range(2)]
        ends_in = [sem(f"ends_in{L}") for L in range(2)]
        out_done = sem("out_done")
        pads_set = sem("pads_set")
        iota_done = sem("iota_done")
        flags_ready = sem("flags_ready")
        keep_set = sem("keep_set")
        consts_ready = sem("consts_ready")
        var_ready = sem("var_ready")
        std_ready = sem("std_ready")
        table_ready = [sem(f"table_ready{L}") for L in range(2)]
        idx_ready = [sem(f"idx_ready{L}") for L in range(2)]
        summed = sem("summed")
        oh_ready = sem("oh_ready")
        hist_mm = sem("hist_mm")
        hist_added = sem("hist_added")
        msg_ready = [sem(f"msg_ready{L}") for L in range(2)]
        carried = [sem(f"carried{L}") for L in range(2)]
        scanned = [sem(f"scanned{L}") for L in range(2)]
        unpacked = [sem(f"unpacked{L}") for L in range(2)]
        cum_mm = sem("cum_mm")
        end_ready = sem("end_ready")
        trail_ready = sem("trail_ready")
        trail_mm = sem("trail_mm")
        carryT_ready = sem("carryT_ready")
        carry_mm = sem("carry_mm")
        carry_ready = sem("carry_ready")
        fix_mm = sem("fix_mm")
        hid_ready = sem("hid_ready")
        hT_mm = sem("hT_mm")
        hT_copied = sem("hT_copied")
        tab_mm = sem("tab_mm")
        tab_copied = sem("tab_copied")
        out_ready = sem("out_ready")
        chunk_begun = sem("chunk_begun")
        dve_step = sem("dve_step")

        block = ctx.enter_context(nc.Block())

        dst_rows = dst[0:(P - 1) * COLS].rearrange("(p t) -> p t", p=P - 1)
        attr_head = edge_attr[0:(P - 1) * COLS, :].rearrange("(p t) f -> p (t f)", p=P - 1)
        attr_full = bass.AP(edge_attr.tensor, 0, [[COLS * D, P], [1, LAST * D]])

        def full_cols(v):
            return bass.AP(v.tensor, 0, [[COLS, P], [1, LAST]])

        def scan_rows(L):
            return scan_d[L].ap().rearrange("(p t) f -> p (t f)", p=P)

        def node_rows(v):
            return v[0:(A - 1) * P, :].rearrange("(a b) f -> b a f", b=P)

        @block.sync
        def _(sp):
            sp.wait_ge(pads_set, 1)
            sp.dma_start(xin[:, 0:A - 1, :], node_rows(x)).then_inc(x_in, 16)
            sp.dma_start(xin[0:NT, A - 1, :], x[(A - 1) * P:N, :]).then_inc(x_in, 16)
            for tile, v in ((src_i, src), (dst_i, dst)):
                head = v[0:(P - 1) * COLS].rearrange("(p t) -> p t", p=P - 1)
                sp.dma_start(tile[:, 0:LAST], full_cols(v)).then_inc(edges_in, 16)
                sp.dma_start(tile[0:P - 1, LAST:COLS], head[:, LAST:COLS]).then_inc(edges_in, 16)
            for s in range(2):
                sp.dma_start(attr[s][:].rearrange("p t f -> p (t f)"),
                             attr_full[:, s * T * D:(s + 1) * T * D]).then_inc(attr_in[s], 16)
            sp.dma_start(eps_t[:], eps.rearrange("(a b) -> a b", a=1).to_broadcast([P, 1])).then_inc(small_in, 16)
            with nc.allow_non_contiguous_dma(reason="one dst of each row"):
                sp.dma_start(edge_i[0:P - 1, 0:1], dst_rows[:, 0:1]).then_inc(small_in, 16)
                sp.dma_start(edge_i[P - 1:P, 0:1], dst[(P - 1) * COLS:(P - 1) * COLS + 1].rearrange("(a b) -> a b", a=1)).then_inc(small_in, 16)
                sp.dma_start(edge_i[1:P, 1:2], dst_rows[:, COLS - 1:COLS]).then_inc(small_in, 16)
                sp.dma_start(edge_i[0:P - 1, 2:3], dst_rows[:, COLS - 1:COLS]).then_inc(small_in, 16)
                sp.dma_start(edge_i[0:P - 2, 3:4], dst_rows[1:P - 1, 0:1]).then_inc(small_in, 16)
                sp.dma_start(edge_i[P - 2:P - 1, 3:4], dst[(P - 1) * COLS:(P - 1) * COLS + 1].rearrange("(a b) -> a b", a=1)).then_inc(small_in, 16)
            sp.dma_start(wcat[0:D, 0:D], phi_t).then_inc(w_in, 16)
            sp.dma_start(wcat[0:D, D:2 * D], theta_t).then_inc(w_in, 16)
            sp.dma_start(wcat[64:65, 0:D], phi_b.rearrange("(a b) -> a b", a=1)).then_inc(w_in, 16)
            sp.dma_start(wcat[64:65, D:2 * D], theta_b.rearrange("(a b) -> a b", a=1)).then_inc(w_in, 16)

            def store_chunk(L, i, s):
                sp.wait_ge(unpacked[L], 2 * i + s + 1)
                sp.dma_start(scan_rows(L)[:, bass.ds((2 * i + s) * T * D, T * D)],
                             rows[s][:].rearrange("p t f -> p (t f)")).then_inc(stored[L][s], 16)

            def store_table(L, tile):
                sp.wait_ge(table_ready[L], 1)
                sp.dma_start(table_d[L].ap().rearrange("(a b) f -> b a f", b=P), tile[:]).then_inc(table_out[L], 16)

            store_table(0, hid)
            with sp.Fori(0, FULL - 1) as i:
                for s in range(2):
                    sp.wait_ge(msg_ready[0], 2 * i + s + 1)
                    sp.dma_start(attr[s][:].rearrange("p t f -> p (t f)"),
                                 attr_full[:, bass.ds((2 * (i + 1) + s) * T * D, T * D)]).then_inc(attr_in[s], 16)
                    store_chunk(0, i, s)
            for s in range(2):
                c = 2 * FULL + s
                left = min(max(LAST - c * T, 0), T)
                sp.wait_ge(msg_ready[0], c - 1)
                flat = attr[s][:].rearrange("p t f -> p (t f)")
                if left:
                    sp.dma_start(flat[:, 0:left * D], attr_full[:, c * T * D:(c * T + left) * D]).then_inc(attr_in[s], 16)
                sp.dma_start(flat[0:P - 1, left * D:T * D],
                             attr_head[:, (c * T + left) * D:(c + 1) * T * D]).then_inc(attr_in[s], 16)
                store_chunk(0, FULL - 1, s)
            for s in range(2):
                store_chunk(0, FULL, s)
            store_table(1, cen)
            with sp.Fori(0, PAIRS) as i:
                for s in range(2):
                    store_chunk(1, i, s)
            sp.wait_ge(out_ready, 1)
            sp.dma_start(node_rows(out), val[:, 0:A - 1, :]).then_inc(out_done, 16)
            sp.dma_start(out[(A - 1) * P:N, :], val[0:NT, A - 1, :]).then_inc(out_done, 16)
            sp.wait_ge(out_done, 32)

        @block.gpsimd
        def _(pool):
            nc.gpsimd.iota(iota_i[:], [[1, P]], base=0, channel_multiplier=0)
            nc.gpsimd.iota(iota_n[:], [[1, A * P]], base=0, channel_multiplier=0)
            nc.gpsimd.iota(pidx_i[:], [[0, 1]], base=0, channel_multiplier=1).then_inc(iota_done, 1)

            def gather_chunk(L, i, s):
                pool.wait_ge(idx_ready[L], 2 * i + s + 1)
                pool.sem_inc(chunk_begun, 1)
                for t in range(T):
                    nc.gpsimd.indirect_dma_start(
                        out=gat[s][:, t, :], out_offset=None, in_=table_d[L].ap(),
                        in_offset=bass.IndirectOffsetOnAxis(ap=idx[s][:, t:t + 1], axis=0),
                    ).then_inc(gathered[L][s], 16)

            for L in range(2):
                pool.wait_ge(table_out[L], 16)
                with pool.Fori(0, PAIRS) as i:
                    for s in range(2):
                        gather_chunk(L, i, s)
                for s in range(2):
                    pool.wait_ge(stored[L][s], 16 * PAIRS)
                pool.wait_ge(end_ready, 1)
                if L == 1:
                    pool.wait_ge(hid_ready, 1)
                for a in range(A):
                    nc.gpsimd.indirect_dma_start(
                        out=val[:, a, :], out_offset=None, in_=scan_d[L].ap(),
                        in_offset=bass.IndirectOffsetOnAxis(ap=end_i[:, a:a + 1], axis=0),
                    ).then_inc(ends_in[L], 16)

        @block.scalar
        def _(act):
            def load_idx(L, i, s):
                nc.scalar.copy(idx[s][:], src_i[:, bass.ds((2 * i + s) * T, T)]).then_inc(idx_ready[L], 1)

            act.wait_ge(edges_in, 64)
            for s in range(2):
                load_idx(0, 0, s)
            act.wait_ge(var_ready, 1)
            nc.scalar.activation(nstat[:, 3, :], nstat[:, 2, :], ACT.Sqrt).then_inc(std_ready, 1)
            act.wait_ge(flags_ready, 1)
            act.wait_ge(keep_set, 1)

            def chunk(L, i, s, more):
                if L == 0:
                    act.wait_ge(summed, 2 * i + s + 1)
                    if more:
                        load_idx(L, i + 1, s)
                    nc.scalar.activation(msg[s][:, :, 1:T + 1].rearrange("p f t -> p t f"), attr[s][:], ACT.Relu)
                    flags = same
                else:
                    act.wait_ge(gathered[L][s], 16 * T * (i + 1))
                    nc.scalar.copy(msg[s][:, :, 1:T + 1].rearrange("p f t -> p t f"), gat[s][:])
                    if more:
                        load_idx(L, i + 1, s)
                    flags = penalty
                nc.scalar.copy(keep[s][:, :, 1:T + 1],
                               flags[:, bass.ds((2 * i + s) * T, T)].unsqueeze(1).to_broadcast([P, D, T])
                               ).then_inc(msg_ready[L], 1)
                act.wait_ge(scanned[L], 2 * i + s + 1)
                nc.scalar.copy(rows[s][:], state[s][:, :, 1:T + 1].rearrange("p f t -> p t f")).then_inc(unpacked[L], 1)

            def rows_free(L, i):
                for s in range(2):
                    act.wait_ge(stored[L][s], 16 * (i + 1))

            with act.Fori(0, PAIRS - 1) as i:
                for s in range(2):
                    chunk(0, i, s, True)
                rows_free(0, i)
            for s in range(2):
                chunk(0, PAIRS - 1, s, False)
            act.wait_ge(var_ready, 2)
            nc.scalar.activation(nstat[:, 3, :], nstat[:, 2, :], ACT.Sqrt).then_inc(std_ready, 1)
            rows_free(0, PAIRS - 1)
            for s in range(2):
                load_idx(1, 0, s)
            act.wait_ge(keep_set, 2)
            with act.Fori(0, PAIRS - 1) as i:
                for s in range(2):
                    chunk(1, i, s, True)
                rows_free(1, i)
            for s in range(2):
                chunk(1, PAIRS - 1, s, False)

        @block.vector
        def _(dve):
            steps = [0]

            def step(ins):
                steps[0] += 1
                ins.then_inc(dve_step, 1)
                dve.wait_ge(dve_step, steps[0])

            def over_features(v):
                return v.unsqueeze(2).to_broadcast([P, A, D])

            def layernorm_relu(n):
                step(nc.vector.tensor_reduce(nstat[:, 0, :], xin[:], AX_X, ALU.add))
                step(nc.vector.tensor_scalar(nstat[:, 1, :], nstat[:, 0, :], 1.0 / D, None, ALU.mult))
                step(nc.vector.tensor_tensor(cen[:], xin[:], over_features(nstat[:, 1, :]), ALU.subtract))
                step(nc.vector.tensor_tensor(hid[:], cen[:], cen[:], ALU.mult))
                step(nc.vector.tensor_reduce(nstat[:, 0, :], hid[:], AX_X, ALU.add))
                nc.vector.tensor_scalar(nstat[:, 2, :], nstat[:, 0, :], 1.0 / D, LN_EPS, ALU.mult, ALU.add).then_inc(var_ready, 1)
                dve.wait_ge(std_ready, n)
                step(nc.vector.reciprocal(nstat[:, 1, :], nstat[:, 3, :]))
                return nc.vector.scalar_tensor_tensor(hid[:], cen[:], 0.0, over_features(nstat[:, 1, :]), ALU.max, ALU.mult)

            nc.vector.memset(edge_i[:], -1)
            nc.vector.memset(wcat[:], 0.0)
            nc.vector.memset(src_i[:, LAST:COLS], 0)
            nc.vector.memset(dst_i[:, LAST:COLS], N)
            nc.vector.memset(xin[:, A - 1, :], 0.0).then_inc(pads_set, 1)
            dve.wait_ge(x_in, 32)
            layernorm_relu(1).then_inc(table_ready[0], 1)

            dve.wait_ge(iota_done, 1)
            nc.vector.tensor_copy(iota_f[:], iota_i[:])
            nc.vector.tensor_copy(iota_b[:], iota_i[:])
            nc.vector.tensor_copy(fixsel[:], iota_n[:])
            nc.vector.memset(ones[:], 1.0)
            nc.vector.memset(hist[:], 0.0)
            nc.vector.memset(hT[:], 0.0)
            for s in range(2):
                nc.vector.memset(keep[s][:, :, 0], 0.0)
            nc.vector.memset(state[1][:, :, T], 0.0)
            nc.vector.memset(carryT[:, 0:1], 0.0)
            nc.vector.memset(carry[:, D:D + 1], 1.0)
            step(nc.vector.tensor_copy(pidx[:], pidx_i[:]))
            nc.vector.tensor_scalar(ident[:], iota_f[:], pidx[:], None, ALU.is_equal)
            nc.vector.tensor_scalar(tri[:], iota_f[:], pidx[:], None, ALU.is_ge)
            nc.vector.memset(hT[64:65, :], 1.0).then_inc(keep_set, 1)
            dve.wait_ge(edges_in, 64)
            nc.vector.memset(same[:, 0:1], 0.0)
            step(nc.vector.tensor_tensor(same[:, 1:COLS], dst_i[:, 1:COLS], dst_i[:, 0:COLS - 1], ALU.is_equal))
            nc.vector.tensor_scalar(penalty[:], same[:], BIG, -BIG, ALU.mult, ALU.add).then_inc(flags_ready, 1)
            lo_i, hi_i = (r[:].rearrange("p t f -> p (t f)").bitcast(I32)[:, 0:COLS] for r in rows)
            step(nc.vector.tensor_scalar(lo_i, dst_i[:], P - 1, None, ALU.bitwise_and))
            step(nc.vector.tensor_scalar(hi_i, dst_i[:], 7, None, ALU.logical_shift_right))
            nc.vector.tensor_copy(dst_lo[:], lo_i)
            step(nc.vector.tensor_copy(dst_hi[:], hi_i))
            dve.wait_ge(small_in, 16 * 7)
            step(nc.vector.tensor_copy(edge[:], edge_i[:]))
            step(nc.vector.tensor_tensor(flag[:, 0:1], edge[:, 0:1], edge[:, 1:2], ALU.is_equal))
            step(nc.vector.tensor_tensor(flag[:, 1:2], edge[:, 0:1], edge[:, 2:3], ALU.is_equal))
            step(nc.vector.tensor_tensor(flag[:, 2:3], edge[:, 0:1], edge[:, 3:4], ALU.is_equal))
            step(nc.vector.tensor_tensor(flag[:, 3:4], flag[:, 0:1], flag[:, 1:2], ALU.mult))
            step(nc.vector.tensor_tensor(flag[:, 4:5], flag[:, 3:4], flag[:, 2:3], ALU.mult))
            step(nc.vector.tensor_tensor(flag[:, 5:6], flag[:, 0:1], flag[:, 4:5], ALU.subtract))
            step(nc.vector.tensor_scalar(flag[:, 6:7], edge[:, 0:1], 1.0, None, ALU.add))
            step(nc.vector.tensor_tensor(flag[:, 6:7], flag[:, 6:7], flag[:, 5:6], ALU.mult))
            step(nc.vector.tensor_scalar(flag[:, 6:7], flag[:, 6:7], -1.0, None, ALU.add))
            step(nc.vector.tensor_scalar(fixsel[:], fixsel[:], flag[:, 6:7], None, ALU.is_equal))
            step(nc.vector.tensor_copy(through[0][:], flag[:, 3:4].to_broadcast([P, D])))
            step(nc.vector.tensor_scalar(through[1][:], through[0][:], BIG, -BIG, ALU.mult, ALU.add))
            step(nc.vector.tensor_scalar(eps_t[:], eps_t[:], 1.0, None, ALU.add))
            dve.wait_ge(w_in, 64)
            nc.vector.tensor_tensor(wcat[0:D, 0:D], wcat[0:D, 0:D], wcat[0:D, D:2 * D], ALU.subtract)
            dve.wait_ge(table_out[0], 16)
            step(nc.vector.scalar_tensor_tensor(xin[:], hid[:], eps_t[:], xin[:], ALU.mult, ALU.add))

            def onehots(i, s):
                cols = bass.ds((2 * i + s) * T, T)
                nc.vector.tensor_tensor(oh_lo[:], iota_b[:].unsqueeze(1).to_broadcast([P, T, P]),
                                        dst_lo[:, cols].unsqueeze(2).to_broadcast([P, T, P]), ALU.is_equal)
                nc.vector.tensor_tensor(oh_hi[:], iota_b[:, 0:A].unsqueeze(1).to_broadcast([P, T, A]),
                                        dst_hi[:, cols].unsqueeze(2).to_broadcast([P, T, A]), ALU.is_equal
                                        ).then_inc(oh_ready, 1)

            def scan_chunk(L, i, s):
                k = 2 * i + s
                dve.wait_ge(msg_ready[L], k + 1)
                nc.vector.tensor_copy(msg[s][:, :, 0], state[1 - s][:, :, T]).then_inc(carried[L], 1)
                dve.wait_ge(carried[L], k + 1)
                ops = (ALU.mult, ALU.add) if L == 0 else (ALU.add, ALU.max)
                flat = [v[s][:].rearrange("p f t -> p (f t)") for v in (state, keep, msg)]
                nc.vector.tensor_tensor_scan(flat[0], flat[1], flat[2], 0.0, *ops).then_inc(scanned[L], 1)
                dve.wait_ge(scanned[L], k + 1)

            def sum_chunk(i, s, attr_dmas):
                dve.wait_ge(gathered[0][s], 16 * T * (i + 1))
                dve.wait_ge(attr_in[s], 16 * (i + attr_dmas))
                nc.vector.tensor_tensor(attr[s][:], attr[s][:], gat[s][:], ALU.add).then_inc(summed, 1)

            def add_hist(i, s):
                k = 2 * i + s
                dve.wait_ge(hist_mm, k + 1)
                nc.vector.tensor_tensor(hist[:], hist[:], ps_hist[:, 0:A], ALU.add).then_inc(hist_added, 1)
                dve.wait_ge(hist_added, k + 1)

            with dve.Fori(0, PAIRS - 1) as i:
                for s in range(2):
                    onehots(i, s)
                    sum_chunk(i, s, 1)
                    add_hist(i, s)
                    scan_chunk(0, i, s)
            for s in range(2):
                i = PAIRS - 1
                onehots(i, s)
                sum_chunk(i, s, 2 if 0 < LAST - (2 * FULL + s) * T < T else 1)
                add_hist(i, s)
                scan_chunk(0, i, s)

            dve.wait_ge(hist_added, CHUNKS)
            step(nc.vector.tensor_scalar(has[:], hist[:], 1.0, None, ALU.min))
            dve.wait_ge(cum_mm, 1)
            step(nc.vector.tensor_copy(cum[:, 0, :], ps_small[:, 32:32 + A]))
            step(nc.vector.tensor_tensor_scan(cum[:, 1, :], ones[:, 0:A], cum[:, 0, :], 0.0, ALU.mult, ALU.add))
            step(nc.vector.tensor_tensor(cum[:, 1, :], cum[:, 1, :], cum[:, 0, :], ALU.subtract))
            step(nc.vector.tensor_tensor(cum[:, 1, :], cum[:, 1, :], ps_small[:, 0:A], ALU.add))
            step(nc.vector.tensor_scalar(cum[:, 2, :], cum[:, 1, :], -1.0, 0.0, ALU.add, ALU.max))
            nc.vector.tensor_copy(end_i[:], cum[:, 2, :]).then_inc(end_ready, 1)

            def stitch(L):
                dve.wait_ge(scanned[L], CHUNKS)
                nc.vector.tensor_copy(trail[:], state[1][:, :, T]).then_inc(trail_ready, 1)
                dve.wait_ge(trail_mm, L + 1)
                nc.vector.tensor_copy(trailT[:], ps_small[0:D, 0:P])
                step(nc.vector.tensor_copy(throughT[L][:], ps_small[0:D, P:2 * P]))
                ops = (ALU.mult, ALU.add) if L == 0 else (ALU.add, ALU.max)
                nc.vector.tensor_tensor_scan(carryT[:, 1:P + 1], throughT[L][:], trailT[:], 0.0, *ops).then_inc(carryT_ready, 1)
                dve.wait_ge(carry_mm, L + 1)
                nc.vector.tensor_copy(carry[:, 0:D], ps_small[:, 0:D]).then_inc(carry_ready, 1)

            def fix(g):
                n = min(PB, A - g * PB)
                return n, ps_fix[:, g, 0:n * (D + 1)].rearrange("p (a f) -> p a f", a=n)

            GROUPS = -(-A // PB)
            stitch(0)
            dve.wait_ge(fix_mm, 1)
            dve.wait_ge(ends_in[0], 16 * A)
            for g in range(GROUPS):
                n, ps = fix(g)
                v = val[:, g * PB:g * PB + n, :]
                step(nc.vector.tensor_tensor(v, v, ps[:, :, 0:D], ALU.add))
            step(nc.vector.tensor_tensor(val[:], val[:], over_features(has[:]), ALU.mult))
            step(nc.vector.tensor_tensor(xin[:], xin[:], val[:], ALU.add))
            layernorm_relu(2).then_inc(hid_ready, 1)

            for g in range(-(-A // 4)):
                n = min(4, A - 4 * g)
                dve.wait_ge(hT_mm, g + 1)
                nc.vector.tensor_copy(hT[0:D, 4 * g * P:(4 * g + n) * P], ps_tab[0:D, g % 2, 0:n * P]).then_inc(hT_copied, 1)
            for g in range(-(-A // TBL)):
                n = min(TBL, A - TBL * g)
                dve.wait_ge(tab_mm, g + 1)
                ps = ps_tab[:, g % 2, 0:n * 2 * D].rearrange("p (a c f) -> p a c f", a=n, c=2)
                nc.vector.tensor_copy(cen[:, TBL * g:TBL * g + n, :], ps[:, :, 0, :])
                last = nc.vector.tensor_copy(atab[:, TBL * g:TBL * g + n, :], ps[:, :, 1, :])
                last.then_inc(tab_copied, 1)
            dve.wait_ge(tab_copied, -(-A // TBL))
            for s in range(2):
                nc.vector.memset(keep[s][:, :, 0], -BIG)
            nc.vector.memset(state[1][:, :, T], 0.0).then_inc(keep_set, 1)
            dve.wait_ge(keep_set, 2)
            nc.vector.memset(fixpen[:], 0.0).then_inc(table_ready[1], 1)

            with dve.Fori(0, PAIRS) as i:
                for s in range(2):
                    scan_chunk(1, i, s)

            stitch(1)
            dve.wait_ge(fix_mm, 2)
            dve.wait_ge(ends_in[1], 16 * A)
            for g in range(GROUPS):
                n, ps = fix(g)
                f = fixpen[:, g * PB:g * PB + n]
                step(nc.vector.tensor_scalar(f, ps[:, :, D], BIG, -BIG, ALU.mult, ALU.add))
                c = cen[:, g * PB:g * PB + n, :]
                step(nc.vector.tensor_tensor(c, ps[:, :, 0:D], f.unsqueeze(2).to_broadcast([P, n, D]), ALU.add))
            step(nc.vector.tensor_tensor(val[:], val[:], cen[:], ALU.max))
            step(nc.vector.tensor_tensor(val[:], val[:], atab[:], ALU.add))
            step(nc.vector.tensor_tensor(val[:], val[:], over_features(has[:]), ALU.mult))
            nc.vector.tensor_tensor(val[:], val[:], xin[:], ALU.add).then_inc(out_ready, 1)

        @block.tensor
        def _(pe):
            def hist_chunk(k):
                pe.wait_ge(oh_ready, k + 1)
                for t in range(T):
                    last = nc.tensor.matmul(ps_hist[:, 0:A], oh_lo[:, t, :], oh_hi[:, t, :],
                                            start=(t == 0), stop=(t == T - 1))
                last.then_inc(hist_mm, 1)
                pe.wait_ge(hist_added, k + 1)

            with pe.Fori(0, CHUNKS) as k:
                hist_chunk(k)
            nc.tensor.matmul(ps_small[:, 0:A], tri[:], hist[:], start=True, stop=True)
            nc.tensor.matmul(ps_small[:, 32:32 + A], ones[:], hist[:], start=True, stop=True).then_inc(cum_mm, 1)

            def stitch(L):
                pe.wait_ge(trail_ready, L + 1)
                if L == 0:
                    pe.wait_ge(end_ready, 1)
                nc.tensor.transpose(ps_small[0:D, 0:P], trail[:], ident[:])
                nc.tensor.transpose(ps_small[0:D, P:2 * P], through[L][:], ident[:]).then_inc(trail_mm, 1)
                pe.wait_ge(carryT_ready, L + 1)
                nc.tensor.transpose(ps_small[:, 0:D], carryT[:, 0:P], ident[0:D, 0:D]).then_inc(carry_mm, 1)
                pe.wait_ge(carry_ready, L + 1)
                for a in range(A):
                    o = (a % PB) * (D + 1)
                    last = nc.tensor.matmul(ps_fix[:, a // PB, o:o + D + 1], fixsel[:, a * P:(a + 1) * P], carry[:],
                                            start=True, stop=True)
                last.then_inc(fix_mm, 1)

            stitch(0)
            pe.wait_ge(hid_ready, 1)
            for g in range(-(-A // 4)):
                if g >= 2:
                    pe.wait_ge(hT_copied, g - 1)
                for a in range(4 * g, min(4 * g + 4, A)):
                    last = nc.tensor.transpose(ps_tab[0:D, g % 2, (a % 4) * P:(a % 4 + 1) * P], hid[:, a, :], ident[:])
                last.then_inc(hT_mm, 1)
            pe.wait_ge(hT_copied, -(-A // 4))
            for g in range(-(-A // TBL)):
                if g >= 2:
                    pe.wait_ge(tab_copied, g - 1)
                for a in range(TBL * g, min(TBL * g + TBL, A)):
                    o = (a % TBL) * 2 * D
                    last = nc.tensor.matmul(ps_tab[:, g % 2, o:o + 2 * D], hT[:, a * P:(a + 1) * P], wcat[:],
                                            start=True, stop=True)
                last.then_inc(tab_mm, 1)
            stitch(1)


def kernel(x, src, dst, edge_attr_48, L0_gnn_eps, L1_gnn_theta_w, L1_gnn_theta_b, L1_gnn_phi_w, L1_gnn_phi_b):
    import numpy as _np
    import concourse.bacc as _bacc
    from concourse import mybir as _mybir
    from concourse.bass_utils import run_bass_kernel_spmd as _run

    ins = {
        "x": x, "src": src, "dst": dst, "edge_attr": edge_attr_48, "eps": L0_gnn_eps,
        "theta_t": _np.asarray(L1_gnn_theta_w).T, "theta_b": L1_gnn_theta_b,
        "phi_t": _np.asarray(L1_gnn_phi_w).T, "phi_b": L1_gnn_phi_b,
    }
    nc = _bacc.Bacc("TRN2", target_bir_lowering=False, num_devices=1)
    arrays, args = {}, []
    for name, a in ins.items():
        a = _np.ascontiguousarray(a)
        arrays[f"in_{name}_dram"] = a
        args.append(nc.dram_tensor(f"in_{name}_dram", a.shape, _mybir.dt.from_np(a.dtype), kind="ExternalInput").ap())
    out = nc.dram_tensor("out_dram", tuple(_np.shape(x)), F32, kind="ExternalOutput").ap()
    gnn_two_layer_kernel(nc, *args, out)
    r = _run(nc, [arrays], core_ids=[0])
    return r.results[0]["out_dram"]
```

```python
from contextlib import ExitStack

import concourse.bass as bass
from concourse import mybir

P = 128
ALU = mybir.AluOpType
ACT = mybir.ActivationFunctionType
F32 = mybir.dt.float32
F16 = mybir.dt.float16
BF16 = mybir.dt.bfloat16
I32 = mybir.dt.int32
AX_X = mybir.AxisListType.X
BIG = 3.0e38
LN_EPS = 1e-5


def gnn_two_layer_kernel(nc, x, src, src_cols, dst, edge_attr, eps, theta_t, theta_b, phi_t, phi_b, out):
    N, D = x.shape
    E = src.shape[0]
    COLS = -(-E // P)
    LAST = E - (P - 1) * COLS
    T = 31
    CHUNKS = COLS // T
    PAIRS = CHUNKS // 2
    A = -(-N // P)
    NT = N - (A - 1) * P
    FULL = (LAST // T) // 2
    assert COLS == CHUNKS * T and CHUNKS == 2 * PAIRS and FULL == PAIRS - 1 and 0 < LAST < COLS
    PB = 10
    TBL = 5

    Q = (11, 12)
    G = tuple(T - q for q in Q)
    SPLITS = 3
    H = -(-A // 2)
    BANK = 4
    BANKS = 3
    ODD = (11, 3)
    KROW = tuple(q * P // odd for q, odd in zip(Q, ODD))
    assert all(q * P % odd == 0 and odd % 2 for q, odd in zip(Q, ODD)) and max(Q) <= BANK * BANKS and H * P <= 2048
    GROUPS = [(0, 5), (5, 9), (9, H)]
    NG = len(GROUPS)
    HALF = COLS // 2

    table_d = [nc.dram_tensor(f"table{L}_d", (A * P, D), F32) for L in range(2)]
    key_d = nc.dram_tensor("key_d", (COLS * P,), F16)
    scan_d = [nc.dram_tensor(f"scan{L}_d", (P * COLS, D), F32) for L in range(2)]

    with ExitStack() as ctx:
        def sb(name, shape, dt=F32):
            return ctx.enter_context(nc.sbuf_tensor(name, shape, dt))

        def psum(name, shape):
            return ctx.enter_context(nc.psum_tensor(name, shape, F32))

        def sem(name):
            return ctx.enter_context(nc.semaphore(name))

        dst_i = sb("dst_i", [P, COLS], I32)
        src_i = sb("src_i", [P, COLS], I32)
        same = sb("same", [P, COLS])
        penalty = sb("penalty", [P, COLS])
        dst_lo = sb("dst_lo", [P, COLS], BF16)
        dst_hi = sb("dst_hi", [P, COLS], BF16)
        mask = sb("mask", [P, COLS, 2], BF16)
        idx = [sb(f"idx{s}", [P, max(G)], I32) for s in range(2)]
        gat = [sb(f"gat{s}", [P, G[0], D]) for s in range(2)]
        attr = [sb(f"attr{s}", [P, T, D]) for s in range(2)]
        msg = sb("msg", [P, D, T + 1])
        keep = sb("keep", [P, D, T + 1])
        state = [sb(f"state{s}", [P, D, T + 1]) for s in range(2)]
        rows = [sb(f"rows{s}", [P, T, D]) for s in range(2)]
        keyraw = [sb(f"keyraw{s}", [P, max(Q) * P], F16) for s in range(2)]
        keyb = [sb(f"keyb{s}", [P, max(Q) * P + 2 * max(ODD)], F16) for s in range(2)]
        onehot = sb("onehot", [P, H, max(Q) * P], BF16)
        parts = sb("parts", [P, H, SPLITS, 2 * D], BF16)
        picked = sb("picked", [P, max(Q), 2, D])
        xin = sb("xin", [P, A, D])
        cen = sb("cen", [P, 2 * H, D])
        hid = sb("hid", [P, 2 * H, D])
        val = sb("val", [P, A, D])
        atab = sb("atab", [P, 2 * H, D])
        nstat = sb("nstat", [P, 4, A])
        spare = onehot[:].rearrange("p h e -> p (h e)").bitcast(F32)
        iota_n = spare[:, 0:A * P].bitcast(I32)
        rowge = spare[:, A * P:2 * A * P]
        hT = spare[0:65, 0:A * P]
        wcat = sb("wcat", [65, 2 * D])
        eps_t = sb("eps_t", [P, 1])
        iota_i = sb("iota_i", [P, P], I32)
        rowsel = sb("rowsel", [P, A * P], BF16)
        fixsel = sb("fixsel", [P, A * P])
        iota_f = sb("iota_f", [P, P])
        iota_b = sb("iota_b", [P, P], BF16)
        node_i = sb("node_i", [P, A], I32)
        pidx_i = sb("pidx_i", [P, 1], I32)
        pidx = sb("pidx", [P, 1])
        ident = sb("ident", [P, P])
        shift = sb("shift", [P, P])
        wrap = sb("wrap", [P, P])
        pidx_b = sb("pidx_b", [P, 1], BF16)
        negj = sb("negj", [P, 1])
        node = sb("node", [P, A])
        signs = sb("signs", [P, 2, A])
        signed = sb("signed", [P, HALF], BF16)
        rowno = sb("rowno", [P, A])
        last = sb("last", [P, 1])
        cum = sb("cum", [P, A])
        scratch = sb("scratch", [P, A])
        has = sb("has", [P, A])
        end_i = sb("end_i", [P, A], I32)
        edge_i = sb("edge_i", [P, 4], I32)
        edge = sb("edge", [P, 4])
        flag = sb("flag", [P, 8])
        through = [sb(f"through{L}", [P, D]) for L in range(2)]
        throughT = [sb(f"throughT{L}", [D, P]) for L in range(2)]
        trail = sb("trail", [P, D])
        trailT = sb("trailT", [D, P])
        carryT = sb("carryT", [D, P + 1])
        carry = sb("carry", [P, D + 1])
        fixpen = sb("fixpen", [P, A])

        ps_gat = [psum(f"ps_gat{s}", [P, BANKS, 512]) for s in range(2)]
        ps_row = psum("ps_row", [P, 512])
        ps_small = psum("ps_small", [P, 512])
        ps_fix, ps_tab = ps_gat

        edges_in = sem("edges_in")
        x_in = sem("x_in")
        cols_in = sem("cols_in")
        key_out = sem("key_out")
        key_in = [[sem(f"key_in{L}{s}") for s in range(2)] for L in range(2)]
        small_in = sem("small_in")
        w_in = sem("w_in")
        attr_in = [sem(f"attr_in{s}") for s in range(2)]
        table_out = [sem(f"table_out{L}") for L in range(2)]
        gathered = [[sem(f"gathered{L}{s}") for s in range(2)] for L in range(2)]
        stored = [[sem(f"stored{L}{s}") for s in range(2)] for L in range(2)]
        ends_in = [sem(f"ends_in{L}") for L in range(2)]
        out_done = sem("out_done")
        pads_set = sem("pads_set")
        iota_done = sem("iota_done")
        flags_ready = sem("flags_ready")
        keep_set = sem("keep_set")
        consts_ready = sem("consts_ready")
        var_ready = sem("var_ready")
        std_ready = sem("std_ready")
        table_ready = [sem(f"table_ready{L}") for L in range(2)]
        idx_ready = [sem(f"idx_ready{L}") for L in range(2)]
        summed = [sem(f"summed{L}") for L in range(2)]
        keys_made = sem("keys_made")
        key_ready = [sem(f"key_ready{L}") for L in range(2)]
        onehot_ready = [sem(f"onehot_ready{L}") for L in range(2)]
        groups_done = [sem(f"groups_done{L}") for L in range(2)]
        psum_read = [sem(f"psum_read{L}") for L in range(2)]
        half_summed = sem("half_summed")
        parts_ready = sem("parts_ready")
        hi_done = sem("hi_done")
        rowsel_ready = sem("rowsel_ready")
        row_mm = sem("row_mm")
        row_read = sem("row_read")
        cum_ready = sem("cum_ready")
        msg_ready = [sem(f"msg_ready{L}") for L in range(2)]
        carried = [sem(f"carried{L}") for L in range(2)]
        scanned = [sem(f"scanned{L}") for L in range(2)]
        unpacked = [sem(f"unpacked{L}") for L in range(2)]
        cum_mm = sem("cum_mm")
        end_ready = sem("end_ready")
        trail_ready = sem("trail_ready")
        trail_mm = sem("trail_mm")
        carryT_ready = sem("carryT_ready")
        carry_mm = sem("carry_mm")
        carry_ready = sem("carry_ready")
        fix_mm = sem("fix_mm")
        hid_ready = sem("hid_ready")
        hT_mm = sem("hT_mm")
        hT_copied = sem("hT_copied")
        tab_mm = sem("tab_mm")
        tab_copied = sem("tab_copied")
        out_ready = sem("out_ready")
        chunk_begun = sem("chunk_begun")
        dve_step = sem("dve_step")

        block = ctx.enter_context(nc.Block())

        dst_rows = dst[0:(P - 1) * COLS].rearrange("(p t) -> p t", p=P - 1)
        attr_head = edge_attr[0:(P - 1) * COLS, :].rearrange("(p t) f -> p (t f)", p=P - 1)
        attr_full = bass.AP(edge_attr.tensor, 0, [[COLS * D, P], [1, LAST * D]])

        def full_cols(v):
            return bass.AP(v.tensor, 0, [[COLS, P], [1, LAST]])

        def scan_rows(L):
            return scan_d[L].ap().rearrange("(p t) f -> p (t f)", p=P)

        def node_rows(v):
            return v[0:(A - 1) * P, :].rearrange("(a b) f -> b a f", b=P)

        @block.sync
        def _(sp):
            sp.wait_ge(pads_set, 1)
            sp.dma_start(xin[:, 0:A - 1, :], node_rows(x)).then_inc(x_in, 16)
            sp.dma_start(xin[0:NT, A - 1, :], x[(A - 1) * P:N, :]).then_inc(x_in, 16)
            sp.dma_start(rows[0][:].rearrange("p t f -> p (t f)").bitcast(I32)[:, 0:COLS],
                         src_cols.rearrange("c p -> (c p)").rearrange("(q c) -> q c", q=P)).then_inc(cols_in, 16)
            for tile, v in ((src_i, src), (dst_i, dst)):
                head = v[0:(P - 1) * COLS].rearrange("(p t) -> p t", p=P - 1)
                sp.dma_start(tile[:, 0:LAST], full_cols(v)).then_inc(edges_in, 16)
                sp.dma_start(tile[0:P - 1, LAST:COLS], head[:, LAST:COLS]).then_inc(edges_in, 16)
            for s in range(2):
                sp.dma_start(attr[s][:].rearrange("p t f -> p (t f)"),
                             attr_full[:, s * T * D:(s + 1) * T * D]).then_inc(attr_in[s], 16)
            sp.dma_start(eps_t[:], eps.rearrange("(a b) -> a b", a=1).to_broadcast([P, 1])).then_inc(small_in, 16)
            last_first = dst[(P - 1) * COLS:(P - 1) * COLS + 1].rearrange("(a b) -> a b", a=1)
            with nc.allow_non_contiguous_dma(reason="one dst of each row"):
                sp.dma_start(edge_i[0:P - 1, 0:1], dst_rows[:, 0:1]).then_inc(small_in, 16)
                sp.dma_start(edge_i[P - 1:P, 0:1], last_first).then_inc(small_in, 16)
                sp.dma_start(edge_i[1:P, 1:2], dst_rows[:, COLS - 1:COLS]).then_inc(small_in, 16)
                sp.dma_start(edge_i[0:P - 1, 2:3], dst_rows[:, COLS - 1:COLS]).then_inc(small_in, 16)
                sp.dma_start(edge_i[0:P - 2, 3:4], dst_rows[1:P - 1, 0:1]).then_inc(small_in, 16)
                sp.dma_start(edge_i[P - 2:P - 1, 3:4], last_first).then_inc(small_in, 16)
            sp.dma_start(wcat[0:D, 0:D], phi_t).then_inc(w_in, 16)
            sp.dma_start(wcat[0:D, D:2 * D], theta_t).then_inc(w_in, 16)
            sp.dma_start(wcat[64:65, 0:D], phi_b.rearrange("(a b) -> a b", a=1)).then_inc(w_in, 16)
            sp.dma_start(wcat[64:65, D:2 * D], theta_b.rearrange("(a b) -> a b", a=1)).then_inc(w_in, 16)

            def load_key(L, k, s):
                sp.dma_start(keyraw[s][:, 0:Q[L] * P],
                             key_d.ap()[bass.ds((k * T + G[L]) * P, Q[L] * P)].unsqueeze(0).to_broadcast([P, Q[L] * P])
                             ).then_inc(key_in[L][s], 16)

            def store_chunk(L, i, s):
                sp.wait_ge(unpacked[L], 2 * i + s + 1)
                sp.dma_start(scan_rows(L)[:, bass.ds((2 * i + s) * T * D, T * D)],
                             rows[s][:].rearrange("p t f -> p (t f)")).then_inc(stored[L][s], 16)

            def store_table(L, tile):
                sp.wait_ge(table_ready[L], 1)
                sp.dma_start(table_d[L].ap().rearrange("(a b) f -> b a f", b=P), tile[:, 0:A, :]).then_inc(table_out[L], 16)

            def next_key(L, i, s):
                sp.wait_ge(key_ready[L], 2 * i + s + 1)
                load_key(L, 2 * i + s + 2, s)

            store_table(0, hid)
            sp.wait_ge(keys_made, 1)
            sp.dma_start(key_d.ap().rearrange("(q c) -> q c", q=P),
                         rows[1][:].rearrange("p t f -> p (t f)").bitcast(F16)[:, 0:COLS]).then_inc(key_out, 16)
            sp.wait_ge(key_out, 16)
            for s in range(2):
                load_key(0, s, s)
            with sp.Fori(0, FULL - 1) as i:
                for s in range(2):
                    next_key(0, i, s)
                    sp.wait_ge(msg_ready[0], 2 * i + s + 1)
                    sp.dma_start(attr[s][:].rearrange("p t f -> p (t f)"),
                                 attr_full[:, bass.ds((2 * (i + 1) + s) * T * D, T * D)]).then_inc(attr_in[s], 16)
                    store_chunk(0, i, s)
            for s in range(2):
                c = 2 * FULL + s
                left = min(max(LAST - c * T, 0), T)
                next_key(0, FULL - 1, s)
                sp.wait_ge(msg_ready[0], c - 1)
                flat = attr[s][:].rearrange("p t f -> p (t f)")
                if left:
                    sp.dma_start(flat[:, 0:left * D], attr_full[:, c * T * D:(c * T + left) * D]).then_inc(attr_in[s], 16)
                sp.dma_start(flat[0:P - 1, left * D:T * D],
                             attr_head[:, (c * T + left) * D:(c + 1) * T * D]).then_inc(attr_in[s], 16)
                store_chunk(0, FULL - 1, s)
            for s in range(2):
                sp.wait_ge(key_ready[0], 2 * FULL + s + 1)
                load_key(1, s, s)
                store_chunk(0, FULL, s)
            store_table(1, cen)
            with sp.Fori(0, PAIRS - 1) as i:
                for s in range(2):
                    next_key(1, i, s)
                    store_chunk(1, i, s)
            for s in range(2):
                store_chunk(1, PAIRS - 1, s)
            sp.wait_ge(out_ready, 1)
            sp.dma_start(node_rows(out), val[:, 0:A - 1, :]).then_inc(out_done, 16)
            sp.dma_start(out[(A - 1) * P:N, :], val[0:NT, A - 1, :]).then_inc(out_done, 16)
            sp.wait_ge(out_done, 32)

        @block.gpsimd
        def _(pool):
            nc.gpsimd.iota(iota_i[:], [[1, P]], base=0, channel_multiplier=0)
            nc.gpsimd.iota(pidx_i[:], [[0, 1]], base=0, channel_multiplier=1)
            nc.gpsimd.iota(iota_n, [[1, A * P]], base=0, channel_multiplier=0)
            nc.gpsimd.iota(node_i[:], [[P, A]], base=0, channel_multiplier=1).then_inc(iota_done, 1)

            def gather_chunk(L, i, s):
                pool.wait_ge(idx_ready[L], 2 * i + s + 1)
                pool.sem_inc(chunk_begun, 1)
                to = gat[s] if L == 0 else attr[s]
                for t in range(G[L]):
                    nc.gpsimd.indirect_dma_start(
                        out=to[:, t, :], out_offset=None, in_=table_d[L].ap(),
                        in_offset=bass.IndirectOffsetOnAxis(ap=idx[s][:, t:t + 1], axis=0),
                    ).then_inc(gathered[L][s], 16)

            for L in range(2):
                pool.wait_ge(table_out[L], 16)
                with pool.Fori(0, PAIRS) as i:
                    for s in range(2):
                        gather_chunk(L, i, s)
                for s in range(2):
                    pool.wait_ge(stored[L][s], 16 * PAIRS)
                pool.wait_ge(end_ready, 1)
                if L == 1:
                    pool.wait_ge(hid_ready, 1)
                for a in range(A):
                    nc.gpsimd.indirect_dma_start(
                        out=val[:, a, :], out_offset=None, in_=scan_d[L].ap(),
                        in_offset=bass.IndirectOffsetOnAxis(ap=end_i[:, a:a + 1], axis=0),
                    ).then_inc(ends_in[L], 16)

        @block.scalar
        def _(act):
            def load_idx(L, i, s):
                nc.scalar.copy(idx[s][:, 0:G[L]], src_i[:, bass.ds((2 * i + s) * T, G[L])]).then_inc(idx_ready[L], 1)

            def rebase_key(L, i, s):
                act.wait_ge(key_in[L][s], 16 * (i + 1))
                w = KROW[L] + 2
                nc.scalar.activation(keyb[s][:, 0:ODD[L] * w].rearrange("p (r c) -> p r c", c=w)[:, :, 0:KROW[L]],
                                     keyraw[s][:, 0:Q[L] * P].rearrange("p (r c) -> p r c", c=KROW[L]),
                                     ACT.Identity, bias=negj[:]).then_inc(key_ready[L], 1)

            act.wait_ge(edges_in, 64)
            for s in range(2):
                load_idx(0, 0, s)
            act.wait_ge(var_ready, 1)
            nc.scalar.activation(nstat[:, 3, :], nstat[:, 2, :], ACT.Sqrt).then_inc(std_ready, 1)
            act.wait_ge(consts_ready, 1)
            for s in range(2):
                rebase_key(0, 0, s)
            for a in range(A):
                for half in range(2):
                    act.wait_ge(row_mm, 2 * a + half + 1)
                    if half == 0:
                        nc.scalar.copy(rowno[:, a:a + 1], ps_row[:, HALF:HALF + 1])
                    if a or half:
                        act.wait_ge(row_read, 2 * a + half)
                    nc.scalar.activation(signed[:], ps_row[:, 0:HALF], ACT.Sign, bias=node[:, a:a + 1], scale=-1.0,
                                         accum_out=signs[:, half, a:a + 1]).then_inc(row_read, 1)

            def rows_free(L, i):
                for s in range(2):
                    act.wait_ge(stored[L][s], 16 * (i + 1))

            def chunk(L, i, s, more):
                act.wait_ge(summed[L], 2 * i + s + 1)
                if L == 1:
                    act.wait_ge(gathered[L][s], 16 * G[L] * (i + 1))
                if L == 0 and more:
                    load_idx(L, i + 1, s)
                nc.scalar.activation(msg[:, :, 1:T + 1].rearrange("p f t -> p t f"), attr[s][:],
                                     ACT.Relu if L == 0 else ACT.Copy)
                flags = same if L == 0 else penalty
                nc.scalar.copy(keep[:, :, 1:T + 1],
                               flags[:, bass.ds((2 * i + s) * T, T)].unsqueeze(1).to_broadcast([P, D, T])
                               ).then_inc(msg_ready[L], 1)
                if more:
                    if L == 1:
                        act.wait_ge(msg_ready[L], 2 * i + s + 1)
                        load_idx(L, i + 1, s)
                    rebase_key(L, i + 1, s)
                act.wait_ge(scanned[L], 2 * i + s + 1)
                nc.scalar.copy(rows[s][:], state[s][:, :, 1:T + 1].rearrange("p f t -> p t f")).then_inc(unpacked[L], 1)

            act.wait_ge(flags_ready, 1)
            act.wait_ge(keep_set, 1)
            act.wait_ge(key_out, 16)
            for L in range(2):
                if L == 1:
                    act.wait_ge(var_ready, 2)
                    nc.scalar.activation(nstat[:, 3, :], nstat[:, 2, :], ACT.Sqrt).then_inc(std_ready, 1)
                    rows_free(0, PAIRS - 1)
                    for s in range(2):
                        load_idx(1, 0, s)
                        rebase_key(1, 0, s)
                    act.wait_ge(keep_set, 2)
                with act.Fori(0, PAIRS - 1) as i:
                    for s in range(2):
                        chunk(L, i, s, True)
                    rows_free(L, i)
                for s in range(2):
                    chunk(L, PAIRS - 1, s, False)

        @block.vector
        def _(dve):
            steps = [0]

            def step(ins):
                steps[0] += 1
                ins.then_inc(dve_step, 1)
                dve.wait_ge(dve_step, steps[0])

            def over_features(v):
                return v.unsqueeze(2).to_broadcast([P, A, D])

            def layernorm_relu(n):
                c, h = cen[:, 0:A, :], hid[:, 0:A, :]
                step(nc.vector.tensor_reduce(nstat[:, 0, :], xin[:], AX_X, ALU.add))
                step(nc.vector.tensor_scalar(nstat[:, 1, :], nstat[:, 0, :], 1.0 / D, None, ALU.mult))
                step(nc.vector.tensor_tensor(c, xin[:], over_features(nstat[:, 1, :]), ALU.subtract))
                step(nc.vector.tensor_tensor(h, c, c, ALU.mult))
                step(nc.vector.tensor_reduce(nstat[:, 0, :], h, AX_X, ALU.add))
                nc.vector.tensor_scalar(nstat[:, 2, :], nstat[:, 0, :], 1.0 / D, LN_EPS, ALU.mult, ALU.add).then_inc(var_ready, 1)
                dve.wait_ge(std_ready, n)
                step(nc.vector.reciprocal(nstat[:, 1, :], nstat[:, 3, :]))
                return nc.vector.scalar_tensor_tensor(h, c, 0.0, over_features(nstat[:, 1, :]), ALU.max, ALU.mult)

            def split_table(tile):
                full = tile[:].rearrange("p (h z) f -> p h (z f)", z=2)
                rest = atab[:].rearrange("p (h z) f -> p h (z f)", z=2)
                for n in range(SPLITS):
                    v = full if n == 0 else rest
                    ins = nc.vector.tensor_copy(parts[:, :, n, :], v)
                    if n == SPLITS - 1:
                        ins.then_inc(parts_ready, 1)
                    else:
                        step(ins)
                        step(nc.vector.tensor_tensor(rest, v, parts[:, :, n, :], ALU.subtract))

            nc.vector.memset(edge_i[:], -1)
            nc.vector.memset(wcat[:], 0.0)
            nc.vector.memset(hid[:, A:2 * H, :], 0.0)
            nc.vector.memset(src_i[:, LAST:COLS], 0)
            nc.vector.memset(dst_i[:, LAST:COLS], N)
            nc.vector.memset(xin[:, A - 1, :], 0.0).then_inc(pads_set, 1)
            dve.wait_ge(x_in, 32)
            layernorm_relu(1).then_inc(table_ready[0], 1)
            dve.wait_ge(table_ready[0], 1)

            dve.wait_ge(iota_done, 1)
            dve.wait_ge(cols_in, 16)
            cols_i, low_i = (r[:].rearrange("p t f -> p (t f)").bitcast(I32)[:, 0:COLS] for r in (rows[0], state[0]))
            keys = rows[1][:].rearrange("p t f -> p (t f)").bitcast(F16)[:, 0:COLS]
            low_i = state[0][:].rearrange("p f t -> p (f t)").bitcast(I32)[:, 0:COLS]
            step(nc.vector.tensor_scalar(low_i, cols_i, P - 1, None, ALU.bitwise_and))
            step(nc.vector.tensor_scalar(cols_i, cols_i, 8, 7, ALU.logical_shift_right, ALU.logical_shift_left))
            nc.vector.tensor_tensor(keys, cols_i, low_i, ALU.add).then_inc(keys_made, 1)
            nc.vector.tensor_copy(iota_f[:], iota_i[:])
            nc.vector.tensor_copy(pidx_b[:], pidx_i[:])
            step(nc.vector.tensor_copy(pidx[:], pidx_i[:]))
            nc.vector.tensor_copy(node[:], node_i[:])
            step(nc.vector.tensor_scalar(negj[:], pidx[:], -1.0, None, ALU.mult))
            step(nc.vector.tensor_scalar(node[:], node[:], 0.5, None, ALU.add))
            nc.vector.tensor_copy(last[:], dst_i[:, COLS - 1:COLS]).then_inc(consts_ready, 1)

            dve.wait_ge(small_in, 16 * 7)
            dve.wait_ge(edges_in, 64)
            step(nc.vector.tensor_copy(edge[:], edge_i[:]))
            step(nc.vector.tensor_copy(last[:], dst_i[:, COLS - 1:COLS]))
            step(nc.vector.tensor_copy(fixsel[:], iota_n))
            step(nc.vector.tensor_scalar(rowge, fixsel[:], edge[:, 1:2], None, ALU.is_ge))
            hi16 = state[1][:].rearrange("p f t -> p (f t)").bitcast(I32)[:, 0:COLS]
            nc.vector.scalar_tensor_tensor(rowsel[:], fixsel[:], last[:], rowge, ALU.is_lt, ALU.mult)
            step(nc.vector.tensor_scalar(low_i, dst_i[:], P - 1, None, ALU.bitwise_and))
            step(nc.vector.tensor_scalar(hi16, dst_i[:], 7, 7, ALU.logical_shift_right, ALU.logical_shift_left))
            nc.vector.tensor_copy(dst_lo[:], low_i)
            nc.vector.tensor_copy(dst_hi[:], hi16).then_inc(rowsel_ready, 1)
            split_table(hid)

            def onehots(L, k, s):
                w = KROW[L] + 2
                key = keyb[s][:, 0:ODD[L] * w].rearrange("p (r c) -> p r c", c=w)[:, :, 0:KROW[L]]
                dve.wait_ge(key_ready[L], k + 1)
                for j, (a, b) in enumerate(GROUPS):
                    dve.wait_ge(groups_done[L], NG * k + j + 1)
                    for h in range(a, b):
                        last_one = nc.vector.tensor_scalar(onehot[:, h, 0:Q[L] * P], key, float(h * P), None, ALU.is_equal)
                    last_one.then_inc(onehot_ready[L], 1)

            dve.sem_inc(psum_read[0], 2)
            dve.sem_inc(psum_read[1], 2)
            onehots(0, 0, 0)

            nc.vector.memset(keep[:, :, 0], 0.0)
            nc.vector.memset(carryT[:, 0:1], 0.0)
            nc.vector.memset(carry[:, D:D + 1], 1.0)
            nc.vector.tensor_scalar(ident[:], iota_f[:], pidx[:], None, ALU.is_equal)
            nc.vector.tensor_scalar(shift[:], iota_f[:], -1.0, pidx[:], ALU.add, ALU.is_equal)
            nc.vector.tensor_scalar(wrap[:], iota_f[:], float(P - 1), pidx[:], ALU.add, ALU.is_equal)
            nc.vector.memset(state[1][:, :, T], 0.0).then_inc(keep_set, 1)
            nc.vector.memset(same[:, 0:1], 0.0)
            step(nc.vector.tensor_tensor(same[:, 1:COLS], dst_i[:, 1:COLS], dst_i[:, 0:COLS - 1], ALU.is_equal))
            nc.vector.tensor_scalar(penalty[:], same[:], BIG, -BIG, ALU.mult, ALU.add).then_inc(flags_ready, 1)
            step(nc.vector.tensor_scalar(low_i, src_i[:], P, 7, ALU.bitwise_and, ALU.logical_shift_right))
            nc.vector.tensor_copy(mask[:, :, 1], low_i)
            nc.vector.tensor_scalar(mask[:, :, 0], low_i, -1.0, 1.0, ALU.mult, ALU.add)
            step(nc.vector.tensor_tensor(flag[:, 0:1], edge[:, 0:1], edge[:, 1:2], ALU.is_equal))
            step(nc.vector.tensor_tensor(flag[:, 1:2], edge[:, 0:1], edge[:, 2:3], ALU.is_equal))
            step(nc.vector.tensor_tensor(flag[:, 2:3], edge[:, 0:1], edge[:, 3:4], ALU.is_equal))
            step(nc.vector.tensor_tensor(flag[:, 3:4], flag[:, 0:1], flag[:, 1:2], ALU.mult))
            step(nc.vector.tensor_tensor(flag[:, 4:5], flag[:, 3:4], flag[:, 2:3], ALU.mult))
            step(nc.vector.tensor_tensor(flag[:, 5:6], flag[:, 0:1], flag[:, 4:5], ALU.subtract))
            step(nc.vector.tensor_scalar(flag[:, 6:7], edge[:, 0:1], 1.0, None, ALU.add))
            step(nc.vector.tensor_tensor(flag[:, 6:7], flag[:, 6:7], flag[:, 5:6], ALU.mult))
            step(nc.vector.tensor_scalar(flag[:, 6:7], flag[:, 6:7], -1.0, None, ALU.add))
            step(nc.vector.tensor_scalar(fixsel[:], fixsel[:], flag[:, 6:7], None, ALU.is_equal))
            step(nc.vector.tensor_copy(through[0][:], flag[:, 3:4].to_broadcast([P, D])))
            step(nc.vector.tensor_scalar(through[1][:], through[0][:], BIG, -BIG, ALU.mult, ALU.add))
            step(nc.vector.tensor_scalar(eps_t[:], eps_t[:], 1.0, None, ALU.add))
            dve.wait_ge(w_in, 64)
            nc.vector.tensor_tensor(wcat[0:D, 0:D], wcat[0:D, 0:D], wcat[0:D, D:2 * D], ALU.subtract)
            step(nc.vector.scalar_tensor_tensor(xin[:], hid[:, 0:A, :], eps_t[:], xin[:], ALU.mult, ALU.add))

            def scan_chunk(L, i, s):
                k = 2 * i + s
                dve.wait_ge(msg_ready[L], k + 1)
                nc.vector.tensor_copy(msg[:, :, 0], state[1 - s][:, :, T]).then_inc(carried[L], 1)
                dve.wait_ge(carried[L], k + 1)
                ops = (ALU.mult, ALU.add) if L == 0 else (ALU.add, ALU.max)
                flat = [v[:].rearrange("p f t -> p (f t)") for v in (state[s], keep, msg)]
                nc.vector.tensor_tensor_scan(flat[0], flat[1], flat[2], 0.0, *ops).then_inc(scanned[L], 1)
                dve.wait_ge(scanned[L], k + 1)

            def pick(L, i, s):
                k = 2 * i + s
                dve.wait_ge(groups_done[L], NG * (k + 2))
                m = mask[:, bass.ds(k * T + G[L], Q[L]), :].rearrange("p q z -> p (q z)")
                for a, b in ((0, Q[L] // BANK), (Q[L] // BANK, -(-Q[L] // BANK))):
                    if a < b:
                        n = min(Q[L] - a * BANK, (b - a) * BANK)
                        c = n // (b - a) * 2
                        ins = nc.vector.tensor_tensor(
                            picked[:, a * BANK:a * BANK + n, :, :].rearrange("p (g q) z f -> p g (q z) f", g=b - a),
                            ps_gat[s][:, a:b, 0:c * D].rearrange("p g (c f) -> p g c f", f=D),
                            m[:, 2 * a * BANK:2 * (a * BANK + n)].rearrange("p (g c) -> p g c", c=c)
                            .unsqueeze(3).to_broadcast([P, b - a, c, D]), ALU.mult)
                ins.then_inc(psum_read[L], 1)
                dve.wait_ge(psum_read[L], k + 3)

            def sum_chunk(L, i, s, attr_dmas):
                k = 2 * i + s
                own = attr[s][:, G[L]:T, :]
                if L == 0:
                    pick(L, i, s)
                    dve.wait_ge(attr_in[s], 16 * (i + attr_dmas))
                    nc.vector.tensor_tensor(own, own, picked[:, 0:Q[L], 0, :], ALU.add).then_inc(half_summed, 1)
                    dve.wait_ge(half_summed, k + 1)
                    nc.vector.tensor_tensor(own, own, picked[:, 0:Q[L], 1, :], ALU.add)
                    dve.wait_ge(gathered[0][s], 16 * G[L] * (i + 1))
                    nc.vector.tensor_tensor(attr[s][:, 0:G[L], :], attr[s][:, 0:G[L], :], gat[s][:], ALU.add).then_inc(summed[L], 1)
                else:
                    pick(L, i, s)
                    nc.vector.tensor_tensor(own, picked[:, 0:Q[L], 0, :], picked[:, 0:Q[L], 1, :], ALU.add).then_inc(summed[L], 1)

            def layer(L):
                with dve.Fori(0, PAIRS - 1) as i:
                    for s in range(2):
                        onehots(L, 2 * i + s + 1, 1 - s)
                        sum_chunk(L, i, s, 1)
                        scan_chunk(L, i, s)
                i = PAIRS - 1
                for s in range(2):
                    if s == 0:
                        onehots(L, 2 * i + 1, 1)
                    sum_chunk(L, i, s, 2 if 0 < LAST - (2 * FULL + s) * T < T else 1)
                    scan_chunk(L, i, s)

            layer(0)

            dve.wait_ge(row_read, 2 * A)
            step(nc.vector.tensor_tensor(cum[:], signs[:, 0, :], signs[:, 1, :], ALU.add))
            step(nc.vector.tensor_scalar(cum[:], cum[:], 0.5, COLS / 2.0, ALU.mult, ALU.add))
            step(nc.vector.tensor_scalar(scratch[:], rowno[:], float(COLS), None, ALU.mult))
            nc.vector.tensor_tensor(cum[:], cum[:], scratch[:], ALU.add).then_inc(cum_ready, 1)
            dve.wait_ge(cum_ready, 1)
            step(nc.vector.tensor_scalar(scratch[:], cum[:], -1.0, 0.0, ALU.add, ALU.max))
            nc.vector.tensor_copy(end_i[:], scratch[:]).then_inc(end_ready, 1)
            dve.wait_ge(cum_mm, 1)
            step(nc.vector.tensor_tensor(has[:], cum[:], ps_row[:, 0:A], ALU.subtract))
            step(nc.vector.tensor_scalar(has[:], has[:], 0.0, 1.0, ALU.max, ALU.min))

            def stitch(L):
                nc.vector.tensor_copy(trail[:], state[1][:, :, T]).then_inc(trail_ready, 1)
                dve.wait_ge(trail_mm, L + 1)
                nc.vector.tensor_copy(trailT[:], ps_small[0:D, 0:P])
                step(nc.vector.tensor_copy(throughT[L][:], ps_small[0:D, P:2 * P]))
                ops = (ALU.mult, ALU.add) if L == 0 else (ALU.add, ALU.max)
                nc.vector.tensor_tensor_scan(carryT[:, 1:P + 1], throughT[L][:], trailT[:], 0.0, *ops).then_inc(carryT_ready, 1)
                dve.wait_ge(carry_mm, L + 1)
                nc.vector.tensor_copy(carry[:, 0:D], ps_small[:, 0:D]).then_inc(carry_ready, 1)

            def fix(g):
                n = min(PB, A - g * PB)
                return n, ps_fix[:, g, 0:n * (D + 1)].rearrange("p (a f) -> p a f", a=n)

            FIXES = -(-A // PB)
            stitch(0)
            dve.wait_ge(fix_mm, 1)
            dve.wait_ge(ends_in[0], 16 * A)
            for g in range(FIXES):
                n, ps = fix(g)
                v = val[:, g * PB:g * PB + n, :]
                step(nc.vector.tensor_tensor(v, v, ps[:, :, 0:D], ALU.add))
            step(nc.vector.tensor_tensor(val[:], val[:], over_features(has[:]), ALU.mult))
            nc.vector.memset(hT, 0.0)
            step(nc.vector.tensor_tensor(xin[:], xin[:], val[:], ALU.add))
            nc.vector.memset(hT[64:65, :], 1.0)
            nc.vector.memset(cen[:, A:2 * H, :], 0.0)
            layernorm_relu(2).then_inc(hid_ready, 1)

            for g in range(-(-A // 4)):
                n = min(4, A - 4 * g)
                dve.wait_ge(hT_mm, g + 1)
                nc.vector.tensor_copy(hT[0:D, 4 * g * P:(4 * g + n) * P], ps_tab[0:D, g % 2, 0:n * P]).then_inc(hT_copied, 1)
            for g in range(-(-A // TBL)):
                n = min(TBL, A - TBL * g)
                dve.wait_ge(tab_mm, g + 1)
                ps = ps_tab[:, g % 2, 0:n * 2 * D].rearrange("p (a c f) -> p a c f", a=n, c=2)
                nc.vector.tensor_copy(cen[:, TBL * g:TBL * g + n, :], ps[:, :, 0, :])
                nc.vector.tensor_copy(hid[:, TBL * g:TBL * g + n, :], ps[:, :, 1, :]).then_inc(tab_copied, 1)
            dve.wait_ge(tab_copied, -(-A // TBL))
            nc.vector.memset(fixpen[:], 0.0).then_inc(table_ready[1], 1)
            split_table(cen)
            dve.wait_ge(parts_ready, 2)
            nc.vector.memset(keep[:, :, 0], -BIG)
            nc.vector.memset(state[1][:, :, T], 0.0).then_inc(keep_set, 1)
            onehots(1, 0, 0)
            layer(1)

            stitch(1)
            dve.wait_ge(fix_mm, 2)
            dve.wait_ge(ends_in[1], 16 * A)
            c = cen[:, 0:A, :]
            for g in range(FIXES):
                n, ps = fix(g)
                f = fixpen[:, g * PB:g * PB + n]
                step(nc.vector.tensor_scalar(f, ps[:, :, D], BIG, -BIG, ALU.mult, ALU.add))
                step(nc.vector.tensor_tensor(cen[:, g * PB:g * PB + n, :], ps[:, :, 0:D],
                                             f.unsqueeze(2).to_broadcast([P, n, D]), ALU.add))
            step(nc.vector.tensor_tensor(val[:], val[:], c, ALU.max))
            step(nc.vector.tensor_tensor(val[:], val[:], hid[:, 0:A, :], ALU.add))
            step(nc.vector.tensor_tensor(val[:], val[:], over_features(has[:]), ALU.mult))
            nc.vector.tensor_tensor(val[:], val[:], xin[:], ALU.add).then_inc(out_ready, 1)

        @block.tensor
        def _(pe):
            pe.wait_ge(consts_ready, 1)
            pe.wait_ge(rowsel_ready, 1)
            for a in range(A):
                for half in range(2):
                    if a or half:
                        pe.wait_ge(row_read, 2 * a + half)
                    sel, cols = rowsel[:, a * P:(a + 1) * P], slice(half * HALF, (half + 1) * HALF)
                    if half == 0:
                        nc.tensor.matmul(ps_row[:, HALF:HALF + 1], sel, pidx_b[:], start=True, stop=True)
                    nc.tensor.matmul(ps_row[:, 0:HALF], sel, dst_lo[:, cols], start=True, stop=False)
                    nc.tensor.matmul(ps_row[:, 0:HALF], sel, dst_hi[:, cols], start=False, stop=True).then_inc(row_mm, 1)

            for L in range(2):
                pe.sem_inc(groups_done[L], NG)

            def gather_chunk(L, i, s):
                k = 2 * i + s
                for j, (a, b) in enumerate(GROUPS):
                    pe.wait_ge(onehot_ready[L], NG * k + j + 1)
                    if j == 0:
                        pe.wait_ge(psum_read[L], k + 1)
                    for h in range(a, b):
                        for q in range(Q[L]):
                            for n in range(SPLITS):
                                o = q % BANK * 2 * D
                                last_one = nc.tensor.matmul(
                                    ps_gat[s][:, q // BANK, o:o + 2 * D], onehot[:, h, q * P:(q + 1) * P], parts[:, h, n, :],
                                    start=(h == 0 and q % BANK == 0 and n == 0),
                                    stop=(h == H - 1 and n == SPLITS - 1 and (q % BANK == BANK - 1 or q == Q[L] - 1)))
                    last_one.then_inc(groups_done[L], 1)

            def layer(L):
                pe.wait_ge(parts_ready, L + 1)
                with pe.Fori(0, PAIRS) as i:
                    for s in range(2):
                        gather_chunk(L, i, s)

            def stitch(L):
                pe.wait_ge(trail_ready, L + 1)
                nc.tensor.transpose(ps_small[0:D, 0:P], trail[:], ident[:])
                nc.tensor.transpose(ps_small[0:D, P:2 * P], through[L][:], ident[:]).then_inc(trail_mm, 1)
                pe.wait_ge(carryT_ready, L + 1)
                nc.tensor.transpose(ps_small[:, 0:D], carryT[:, 0:P], ident[0:D, 0:D]).then_inc(carry_mm, 1)
                pe.wait_ge(carry_ready, L + 1)
                for a in range(A):
                    o = (a % PB) * (D + 1)
                    last_one = nc.tensor.matmul(ps_fix[:, a // PB, o:o + D + 1], fixsel[:, a * P:(a + 1) * P], carry[:],
                                                start=True, stop=True)
                last_one.then_inc(fix_mm, 1)

            layer(0)
            pe.wait_ge(cum_ready, 1)
            nc.tensor.matmul(ps_row[:, 0:A], shift[:], cum[:], start=True, stop=False)
            nc.tensor.matmul(ps_row[:, 1:A], wrap[:], cum[:, 0:A - 1], start=False, stop=True).then_inc(cum_mm, 1)
            stitch(0)
            pe.wait_ge(hid_ready, 1)
            for g in range(-(-A // 4)):
                if g >= 2:
                    pe.wait_ge(hT_copied, g - 1)
                for a in range(4 * g, min(4 * g + 4, A)):
                    last_one = nc.tensor.transpose(ps_tab[0:D, g % 2, (a % 4) * P:(a % 4 + 1) * P], hid[:, a, :], ident[:])
                last_one.then_inc(hT_mm, 1)
            pe.wait_ge(hT_copied, -(-A // 4))
            for g in range(-(-A // TBL)):
                if g >= 2:
                    pe.wait_ge(tab_copied, g - 1)
                for a in range(TBL * g, min(TBL * g + TBL, A)):
                    o = (a % TBL) * 2 * D
                    last_one = nc.tensor.matmul(ps_tab[:, g % 2, o:o + 2 * D], hT[:, a * P:(a + 1) * P], wcat[:],
                                                start=True, stop=True)
                last_one.then_inc(tab_mm, 1)
            layer(1)
            stitch(1)


def kernel(x, src, dst, edge_attr_48, L0_gnn_eps, L1_gnn_theta_w, L1_gnn_theta_b, L1_gnn_phi_w, L1_gnn_phi_b):
    import numpy as _np
    import concourse.bacc as _bacc
    from concourse import mybir as _mybir
    from concourse.bass_utils import run_bass_kernel_spmd as _run

    src = _np.asarray(src)
    runs = _np.zeros((P, -(-src.shape[0] // P)), src.dtype)
    runs.reshape(-1)[: src.shape[0]] = src
    ins = {
        "x": x, "src": src, "src_cols": runs.T, "dst": dst, "edge_attr": edge_attr_48, "eps": L0_gnn_eps,
        "theta_t": _np.asarray(L1_gnn_theta_w).T, "theta_b": L1_gnn_theta_b,
        "phi_t": _np.asarray(L1_gnn_phi_w).T, "phi_b": L1_gnn_phi_b,
    }
    nc = _bacc.Bacc("TRN2", target_bir_lowering=False, num_devices=1)
    arrays, args = {}, []
    for name, a in ins.items():
        a = _np.ascontiguousarray(a)
        arrays[f"in_{name}_dram"] = a
        args.append(nc.dram_tensor(f"in_{name}_dram", a.shape, _mybir.dt.from_np(a.dtype), kind="ExternalInput").ap())
    out = nc.dram_tensor("out_dram", tuple(_np.shape(x)), F32, kind="ExternalOutput").ap()
    gnn_two_layer_kernel(nc, *args, out)
    r = _run(nc, [arrays], core_ids=[0])
    return r.results[0]["out_dram"]
```

```python
from contextlib import ExitStack

import concourse.bass as bass
from concourse import mybir

P = 128
ALU = mybir.AluOpType
ACT = mybir.ActivationFunctionType
F32 = mybir.dt.float32
F16 = mybir.dt.float16
BF16 = mybir.dt.bfloat16
I32 = mybir.dt.int32
AX_X = mybir.AxisListType.X
BIG = 3.0e38
LN_EPS = 1e-5


def gnn_two_layer_kernel(nc, x, src, src_cols, dst, edge_attr, eps, theta_t, theta_b, phi_t, phi_b, out):
    N, D = x.shape
    E = src.shape[0]
    COLS = -(-E // P)
    LAST = E - (P - 1) * COLS
    T = 31
    CHUNKS = COLS // T
    PAIRS = CHUNKS // 2
    A = -(-N // P)
    NT = N - (A - 1) * P
    FULL = (LAST // T) // 2
    assert COLS == CHUNKS * T and CHUNKS == 2 * PAIRS and FULL == PAIRS - 1 and 0 < LAST < COLS
    HALVES = ((0, T // 2), (T // 2, T))
    PB = 8
    TBL = 4

    Q = ((12, 12), (12, 12))
    G = tuple(tuple(T - q for q in pair) for pair in Q)
    EXTRA = 1
    QMAX = max(q for pair in Q for q in pair)
    SPLITS = 3
    H = -(-A // 2)
    BANK = 4
    BANKS = 3
    def odd_rows(q):
        return q // (q & -q)

    assert all(odd_rows(q) > 1 for pair in Q for q in pair) and QMAX <= BANK * BANKS and H * P <= 2048
    FIRST = [(0, H - H % 2), (H - H % 2, A)]
    WHOLE = A // PB * PB
    NODES = [(a, a + PB) for a in range(0, WHOLE - PB, PB)]
    NODES += [(a, min(a + TBL, A)) for a in range(WHOLE - PB, A, TBL)]
    GROUPS = [(0, 2), (2, 5), (5, 9), (9, H)]
    NG = len(GROUPS)
    WITH_SECOND = min(j for j, (_, h) in enumerate(GROUPS) if 2 * h > FIRST[0][1])
    CENTRE = N // 2
    assert N - CENTRE <= 2048
    HALF = COLS // 2
    A2 = 2 * H
    assert A <= CHUNKS <= A2
    table_d = [nc.dram_tensor(f"table{L}_d", (A * P, D), F32) for L in range(2)]
    key_d = nc.dram_tensor("key_d", (COLS * P,), F16)
    scan_d = [nc.dram_tensor(f"scan{L}_d", (P * COLS, D), F32) for L in range(2)]

    with ExitStack() as ctx:
        def sb(name, shape, dt=F32):
            return ctx.enter_context(nc.sbuf_tensor(name, shape, dt))

        def psum(name, shape):
            return ctx.enter_context(nc.psum_tensor(name, shape, F32))

        def sem(name):
            return ctx.enter_context(nc.semaphore(name))

        dst_i = sb("dst_i", [P, COLS], I32)
        src_i = sb("src_i", [P, COLS], I32)
        same = sb("same", [P, COLS])
        dst_c = sb("dst_c", [P, COLS], F16)
        mask = sb("mask", [P, COLS, 2], BF16)
        idx = [sb(f"idx{s}", [P, T], I32) for s in range(2)]
        gat = [sb(f"gat{s}", [P, G[0][s] + s * EXTRA, D]) for s in range(2)]
        attr = [sb(f"attr{s}", [P, T, D]) for s in range(2)]
        msg = sb("msg", [P, D, T + 1])
        keep = sb("keep", [P, D, T + 1])
        state = [sb(f"state{s}", [P, D, T + 1]) for s in range(2)]
        rows = [sb(f"rows{s}", [P, T, D]) for s in range(2)]
        keyraw = [sb(f"keyraw{s}", [P, QMAX * P], F16) for s in range(2)]
        keyb = [sb(f"keyb{s}", [P, QMAX * (P + 2)], F16) for s in range(2)]
        onehot = sb("onehot", [P, H, QMAX * P], BF16)
        parts = sb("parts", [P, H, SPLITS, 2 * D], BF16)
        picked = sb("picked", [P, QMAX, 2, D])
        xin = sb("xin", [P, A, D])
        cen = sb("cen", [P, 2 * H, D])
        hid = sb("hid", [P, 2 * H, D])
        val = sb("val", [P, A, D])
        atab = sb("atab", [P, 2 * H, D])
        nstat = sb("nstat", [P, 4, A])
        hT = [sb(f"hT{g}", [65, PB * P]) for g in range(2)]
        wcat = sb("wcat", [65, 2 * D])
        eps_t = sb("eps_t", [P, 1])
        ln_eps = sb("ln_eps", [P, 1])
        rowsel = sb("rowsel", [P, A2 * P], F16)
        fixsel = sb("fixsel", [P, A2 * P])
        iota_f = sb("iota_f", [P, P])
        pidx = sb("pidx", [P, 1])
        ident = sb("ident", [P, P])
        shift = sb("shift", [P, P])
        wrap = sb("wrap", [P, P])
        pidx_h = sb("pidx_h", [P, 1], F16)
        negj = sb("negj", [P, 1])
        node = sb("node", [P, A2])
        signs = sb("signs", [P, 2, A2])
        signed = sb("signed", [P, HALF], BF16)
        rowno = sb("rowno", [P, A2])
        last = sb("last", [P, 1])
        cum = sb("cum", [P, A])
        scratch = sb("scratch", [P, A])
        has = sb("has", [P, A])
        end_i = sb("end_i", [P, A], I32)
        edge_i = sb("edge_i", [P, 4], I32)
        edge = sb("edge", [P, 4])
        flag = sb("flag", [P, 8])
        through = [sb(f"through{L}", [P, D]) for L in range(2)]
        throughT = [sb(f"throughT{L}", [D, P]) for L in range(2)]
        trail = sb("trail", [P, D])
        trailT = sb("trailT", [D, P])
        carryT = sb("carryT", [D, P + 1])
        carry = sb("carry", [P, D + 1])
        fixpen = sb("fixpen", [P, A])

        banks = psum("banks", [P, 8, 512])
        ps_gat = [banks[:, BANKS * s:BANKS * (s + 1), :] for s in range(2)]
        ps_row, ps_small = banks[:, 6, :], banks[:, 7, :]
        ps_fix = banks[:, 0:4, :]
        ps_hT = [banks[:, 4:6, :], banks[:, 0:2, :]]
        ps_tab = [banks[:, 6:8, :], banks[:, 2:4, :]]

        edges_in = sem("edges_in")
        x_in = [sem(f"x_in{g}") for g in range(2)]
        cols_in = sem("cols_in")
        key_out = sem("key_out")
        key_in = [[sem(f"key_in{L}{s}") for s in range(2)] for L in range(2)]
        small_in = sem("small_in")
        w_in = sem("w_in")
        attr_in = [sem(f"attr_in{s}") for s in range(2)]
        table_out = [sem(f"table_out{L}") for L in range(2)]
        gathered = [[sem(f"gathered{L}{s}") for s in range(2)] for L in range(2)]
        stored = [[sem(f"stored{L}{s}") for s in range(2)] for L in range(2)]
        ends_in = [[sem(f"ends_in{L}{g}") for g in range(len(NODES))] for L in range(2)]
        out_done = sem("out_done")
        pads_set = sem("pads_set")
        iota_done = sem("iota_done")
        numbers_done = sem("numbers_done")
        flags_ready = sem("flags_ready")
        keep_set = sem("keep_set")
        consts_ready = sem("consts_ready")
        squares_ready = sem("squares_ready")
        std_ready = sem("std_ready")
        table_ready = [sem(f"table_ready{L}") for L in range(2)]
        idx_ready = [sem(f"idx_ready{L}") for L in range(2)]
        summed = [sem(f"summed{L}") for L in range(2)]
        keys_made = sem("keys_made")
        key_ready = [sem(f"key_ready{L}") for L in range(2)]
        onehot_ready = [sem(f"onehot_ready{L}") for L in range(2)]
        groups_done = [sem(f"groups_done{L}") for L in range(2)]
        psum_read = [sem(f"psum_read{L}") for L in range(2)]
        half_summed = sem("half_summed")
        part_cast = [[sem(f"part{n}_cast{L}") for n in range(SPLITS)] for L in range(2)]
        rest_ready = [[sem(f"rest{n}_ready{L}") for n in range(SPLITS - 1)] for L in range(2)]
        rowsel_ready = sem("rowsel_ready")
        row_mm = sem("row_mm")
        row_read = sem("row_read")
        cum_ready = sem("cum_ready")
        msg_ready = [sem(f"msg_ready{L}") for L in range(2)]
        carried = [sem(f"carried{L}") for L in range(2)]
        scanned = [sem(f"scanned{L}") for L in range(2)]
        unpacked = [sem(f"unpacked{L}") for L in range(2)]
        cum_mm = sem("cum_mm")
        end_ready = sem("end_ready")
        trail_ready = sem("trail_ready")
        trail_mm = sem("trail_mm")
        carryT_ready = sem("carryT_ready")
        carry_mm = sem("carry_mm")
        carry_ready = sem("carry_ready")
        fix_mm = sem("fix_mm")
        hid_ready = sem("hid_ready")
        hT_mm = sem("hT_mm")
        hT_copied = sem("hT_copied")
        tab_mm = sem("tab_mm")
        out_ready = sem("out_ready")
        chunk_begun = sem("chunk_begun")
        dve_step = sem("dve_step")
        blocks_ready = sem("blocks_ready")
        masks_ready = sem("masks_ready")
        hT_set = sem("hT_set")

        block = ctx.enter_context(nc.Block())

        dst_rows = dst[0:(P - 1) * COLS].rearrange("(p t) -> p t", p=P - 1)
        attr_head = edge_attr[0:(P - 1) * COLS, :].rearrange("(p t) f -> p (t f)", p=P - 1)
        attr_full = bass.AP(edge_attr.tensor, 0, [[COLS * D, P], [1, LAST * D]])

        def full_cols(v):
            return bass.AP(v.tensor, 0, [[COLS, P], [1, LAST]])

        def scan_rows(L):
            return scan_d[L].ap().rearrange("(p t) f -> p (t f)", p=P)

        def node_rows(v):
            return v[0:(A - 1) * P, :].rearrange("(a b) f -> b a f", b=P)

        def key_view(L, s):
            rows_ = odd_rows(Q[L][s])
            w = Q[L][s] * P // rows_
            return keyb[s][:, 0:rows_ * (w + 2)].rearrange("p (r c) -> p r c", c=w + 2)[:, :, 0:w]

        def pair_view(tile, a, b):
            return tile[:, a:b + b % 2, :].rearrange("p (h z) f -> p h (z f)", z=2)

        block_i = msg[:].rearrange("p f t -> p (f t)").bitcast(I32)[:, 0:COLS]

        @block.sync
        def _(sp):
            sp.dma_start(rows[0][:].rearrange("p t f -> p (t f)").bitcast(I32)[:, 0:COLS],
                         src_cols.rearrange("c p -> (c p)").rearrange("(q c) -> q c", q=P)).then_inc(cols_in, 16)
            cut = FIRST[0][1]
            sp.dma_start(xin[:, 0:cut, :], node_rows(x)[:, 0:cut, :]).then_inc(x_in[0], 16)
            sp.dma_start(xin[:, cut:A - 1, :], node_rows(x)[:, cut:A - 1, :]).then_inc(x_in[1], 16)
            sp.wait_ge(pads_set, 1)
            sp.dma_start(xin[0:NT, A - 1, :], x[(A - 1) * P:N, :]).then_inc(x_in[1], 16)
            for tile, v in ((src_i, src), (dst_i, dst)):
                head = v[0:(P - 1) * COLS].rearrange("(p t) -> p t", p=P - 1)
                sp.dma_start(tile[:, 0:LAST], full_cols(v)).then_inc(edges_in, 16)
                sp.dma_start(tile[0:P - 1, LAST:COLS], head[:, LAST:COLS]).then_inc(edges_in, 16)
                if tile is src_i:
                    sp.wait_ge(keys_made, 1)
                    sp.dma_start(key_d.ap().rearrange("(q c) -> q c", q=P),
                                 rows[1][:].rearrange("p t f -> p (t f)").bitcast(F16)[:, 0:COLS]).then_inc(key_out, 16)

            def load_key(L, k, s):
                n = Q[L][s] * P
                sp.dma_start(keyraw[s][:, 0:n], key_d.ap()[bass.ds((k * T + G[L][s]) * P, n)].unsqueeze(0).to_broadcast([P, n])
                             ).then_inc(key_in[L][s], 16)

            sp.wait_ge(key_out, 16)
            for s in range(2):
                load_key(0, s, s)
            def store_table(L, tile, a, b, n):
                sp.wait_ge(table_ready[L], n)
                sp.dma_start(table_d[L].ap().rearrange("(a b) f -> b a f", b=P)[:, a:b, :], tile[:, a:b, :]
                             ).then_inc(table_out[L], 16)

            def first_attr(s):
                sp.dma_start(attr[s][:].rearrange("p t f -> p (t f)"),
                             attr_full[:, s * T * D:(s + 1) * T * D]).then_inc(attr_in[s], 16)

            store_table(0, hid, *FIRST[0], 1)
            first_attr(0)
            sp.dma_start(eps_t[:], eps.rearrange("(a b) -> a b", a=1).to_broadcast([P, 1])).then_inc(small_in, 16)
            last_first = dst[(P - 1) * COLS:(P - 1) * COLS + 1].rearrange("(a b) -> a b", a=1)
            with nc.allow_non_contiguous_dma(reason="one dst of each row"):
                sp.dma_start(edge_i[0:P - 1, 0:1], dst_rows[:, 0:1]).then_inc(small_in, 16)
                sp.dma_start(edge_i[P - 1:P, 0:1], last_first).then_inc(small_in, 16)
                sp.dma_start(edge_i[1:P, 1:2], dst_rows[:, COLS - 1:COLS]).then_inc(small_in, 16)
                sp.dma_start(edge_i[0:P - 1, 2:3], dst_rows[:, COLS - 1:COLS]).then_inc(small_in, 16)
                sp.dma_start(edge_i[0:P - 2, 3:4], dst_rows[1:P - 1, 0:1]).then_inc(small_in, 16)
                sp.dma_start(edge_i[P - 2:P - 1, 3:4], last_first).then_inc(small_in, 16)
            store_table(0, hid, *FIRST[1], 2)
            first_attr(1)
            sp.dma_start(wcat[0:D, 0:D], phi_t).then_inc(w_in, 16)
            sp.dma_start(wcat[0:D, D:2 * D], theta_t).then_inc(w_in, 16)
            sp.dma_start(wcat[64:65, 0:D], phi_b.rearrange("(a b) -> a b", a=1)).then_inc(w_in, 16)
            sp.dma_start(wcat[64:65, D:2 * D], theta_b.rearrange("(a b) -> a b", a=1)).then_inc(w_in, 16)

            def store_chunk(L, i, s, t0=0, t1=T, more=0):
                sp.wait_ge(unpacked[L], 2 * i + s + 1 + more)
                sp.dma_start(scan_rows(L)[:, bass.ds(((2 * i + s) * T + t0) * D, (t1 - t0) * D)],
                             rows[s][:, t0:t1, :].rearrange("p t f -> p (t f)")).then_inc(stored[L][s], 16)

            def store_last_chunks(L):
                store_chunk(L, PAIRS - 1, 0)
                for n in range(2):
                    store_chunk(L, PAIRS - 1, 1, *HALVES[n], n)

            def next_key(L, i, s):
                sp.wait_ge(key_ready[L], 2 * i + s + 1)
                load_key(L, 2 * i + s + 2, s)

            with sp.Fori(0, FULL - 1) as i:
                for s in range(2):
                    next_key(0, i, s)
                    sp.wait_ge(msg_ready[0], 2 * i + s + 1)
                    sp.dma_start(attr[s][:].rearrange("p t f -> p (t f)"),
                                 attr_full[:, bass.ds((2 * (i + 1) + s) * T * D, T * D)]).then_inc(attr_in[s], 16)
                    store_chunk(0, i, s)
            for s in range(2):
                c = 2 * FULL + s
                left = min(max(LAST - c * T, 0), T)
                next_key(0, FULL - 1, s)
                sp.wait_ge(msg_ready[0], c - 1)
                flat = attr[s][:].rearrange("p t f -> p (t f)")
                if left:
                    sp.dma_start(flat[:, 0:left * D], attr_full[:, c * T * D:(c * T + left) * D]).then_inc(attr_in[s], 16)
                sp.dma_start(flat[0:P - 1, left * D:T * D],
                             attr_head[:, (c * T + left) * D:(c + 1) * T * D]).then_inc(attr_in[s], 16)
                store_chunk(0, FULL - 1, s)
            for s in range(2):
                sp.wait_ge(key_ready[0], 2 * FULL + s + 1)
                load_key(1, s, s)
            store_last_chunks(0)
            for g, (a, b) in enumerate(NODES):
                store_table(1, cen, a, b, g + 1)
            with sp.Fori(0, PAIRS - 1) as i:
                for s in range(2):
                    next_key(1, i, s)
                    store_chunk(1, i, s)
            store_last_chunks(1)
            for g, (a, b) in enumerate(NODES):
                sp.wait_ge(out_ready, g + 1)
                if a < A - 1:
                    e = min(b, A - 1)
                    sp.dma_start(node_rows(out)[:, a:e, :], val[:, a:e, :]).then_inc(out_done, 16)
                if b == A:
                    sp.dma_start(out[(A - 1) * P:N, :], val[0:NT, A - 1, :]).then_inc(out_done, 16)
            sp.wait_ge(out_done, 16 * (sum(a < A - 1 for a, _ in NODES) + 1))

        @block.gpsimd
        def _(pool):
            nc.gpsimd.iota(pidx[:], [[0, 1]], base=0, channel_multiplier=1, allow_small_or_imprecise_dtypes=True)
            nc.gpsimd.iota(iota_f[:], [[1, P]], base=0, channel_multiplier=0, allow_small_or_imprecise_dtypes=True)
            nc.gpsimd.iota(node[:], [[P, A2]], base=0, channel_multiplier=1, allow_small_or_imprecise_dtypes=True
                           ).then_inc(iota_done, 1)
            nc.gpsimd.iota(fixsel[:], [[1, A2 * P]], base=0, channel_multiplier=0, allow_small_or_imprecise_dtypes=True
                           ).then_inc(numbers_done, 1)

            for g in range(2):
                nc.gpsimd.memset(hT[g][:], 0.0).then_inc(hT_set, 1)
                pool.wait_ge(hT_set, 2 * g + 1)
                nc.gpsimd.memset(hT[g][64:65, :], 1.0).then_inc(hT_set, 1)
                pool.wait_ge(hT_set, 2 * g + 2)

            pool.wait_ge(blocks_ready, 1)
            nc.gpsimd.tensor_copy(mask[:, :, 1], block_i)
            nc.gpsimd.tensor_scalar(mask[:, :, 0], block_i, -1.0, 1.0, ALU.mult, ALU.add).then_inc(masks_ready, 1)

            def gather_chunk(L, i, s, extra=0):
                pool.wait_ge(idx_ready[L], 2 * i + s + 1)
                pool.sem_inc(chunk_begun, 1)
                to = gat[s] if L == 0 else attr[s]
                for n, t in enumerate([*range(G[L][s]), *range(T - extra, T)]):
                    nc.gpsimd.indirect_dma_start(
                        out=to[:, n, :], out_offset=None, in_=table_d[L].ap(),
                        in_offset=bass.IndirectOffsetOnAxis(ap=idx[s][:, t:t + 1], axis=0),
                    ).then_inc(gathered[L][s], 16)

            for L in range(2):
                pool.wait_ge(table_out[L], 16 * len((FIRST, NODES)[L]))
                with pool.Fori(0, PAIRS - 1) as i:
                    for s in range(2):
                        gather_chunk(L, i, s)
                gather_chunk(L, PAIRS - 1, 0)
                gather_chunk(L, PAIRS - 1, 1, (EXTRA, 0)[L])
                for s in range(2):
                    pool.wait_ge(stored[L][s], 16 * (PAIRS + 1 + s))
                pool.wait_ge(end_ready, 1)
                if L == 1:
                    pool.wait_ge(hid_ready, len(NODES))
                for g, (a0, a1) in enumerate(NODES):
                    for a in range(a0, a1):
                        nc.gpsimd.indirect_dma_start(
                            out=val[:, a, :], out_offset=None, in_=scan_d[L].ap(),
                            in_offset=bass.IndirectOffsetOnAxis(ap=end_i[:, a:a + 1], axis=0),
                        ).then_inc(ends_in[L][g], 16)

        @block.scalar
        def _(act):
            def load_idx(L, i, s):
                nc.scalar.copy(idx[s][:], src_i[:, bass.ds((2 * i + s) * T, T)]).then_inc(idx_ready[L], 1)

            def rebase_key(L, i, s):
                act.wait_ge(key_in[L][s], 16 * (i + 1))
                nc.scalar.activation(key_view(L, s), keyraw[s][:, 0:Q[L][s] * P].rearrange("p (r c) -> p r c", r=odd_rows(Q[L][s])),
                                     ACT.Identity, bias=negj[:]).then_inc(key_ready[L], 1)

            def root(n, a, b):
                act.wait_ge(squares_ready, n)
                nc.scalar.activation(nstat[:, 3, a:b], nstat[:, 2, a:b], ACT.Sqrt, bias=ln_eps[:], scale=1.0 / D
                                     ).then_inc(std_ready, 1)

            def cast_part(L, g, n, tile, a, b):
                if n:
                    act.wait_ge(rest_ready[L][n - 1], g + 1)
                nc.scalar.copy(parts[:, a // 2:-(-b // 2), n, :], pair_view(tile if n == 0 else atab, a, b)
                               ).then_inc(part_cast[L][n], 1)

            def count_row(k, half):
                act.wait_ge(row_mm, 2 * k + half + 1)
                if half == 0:
                    nc.scalar.copy(rowno[:, bass.ds(k, 1)], ps_row[:, HALF:HALF + 1])
                act.wait_ge(row_read, 2 * k + half + 1)
                nc.scalar.activation(signed[:], ps_row[:, 0:HALF], ACT.Sign, bias=node[:, bass.ds(k, 1)], scale=-1.0,
                                     accum_out=signs[:, half, bass.ds(k, 1)]).then_inc(row_read, 1)

            act.sem_inc(row_read, 1)
            for L in range(2):
                for s in range(2):
                    act.sem_inc(stored[L][s], 16)
            act.wait_ge(iota_done, 1)
            nc.scalar.activation(scratch[:, 0:1], pidx[:], ACT.Sqrt)
            root(1, *FIRST[0])
            act.wait_ge(consts_ready, 1)
            rebase_key(0, 0, 0)
            act.wait_ge(edges_in, 64)
            for s in range(2):
                load_idx(0, 0, s)
            root(2, *FIRST[1])
            for g, (a, b) in enumerate(FIRST):
                act.wait_ge(table_ready[0], g + 1)
                for n in range(SPLITS):
                    cast_part(0, g, n, hid, a, b)
            rebase_key(0, 0, 1)

            def chunk(L, i, s, more):
                k = 2 * i + s
                nc.scalar.activation(keep[:, :, 1:T + 1], same[:, bass.ds(k * T, T)].unsqueeze(1).to_broadcast([P, D, T]), ACT.Copy,
                                     scale=(1.0, BIG)[L], bias=(0.0, -BIG)[L])
                if L == 0:
                    count_row(k, 0)
                act.wait_ge(summed[L], k + 1)
                if L == 1:
                    act.wait_ge(gathered[L][s], 16 * G[L][s] * (i + 1))
                if L == 0 and more:
                    load_idx(L, i + 1, s)
                nc.scalar.activation(msg[:, :, 1:T + 1].rearrange("p f t -> p t f"), attr[s][:],
                                     ACT.Relu if L == 0 else ACT.Copy).then_inc(msg_ready[L], 1)
                if L == 0:
                    count_row(k, 1)
                if more:
                    if L == 1:
                        act.wait_ge(msg_ready[L], k + 1)
                        load_idx(L, i + 1, s)
                    rebase_key(L, i + 1, s)
                act.wait_ge(scanned[L], k + 1)
                act.wait_ge(stored[L][s], 16 * (i + 1))
                for t0, t1 in HALVES if s == 1 and not more else ((0, T),):
                    nc.scalar.copy(rows[s][:, t0:t1, :], state[s][:, :, t0 + 1:t1 + 1].rearrange("p f t -> p t f")
                                   ).then_inc(unpacked[L], 1)

            def chunks(L):
                with act.Fori(0, PAIRS - 1) as i:
                    for s in range(2):
                        chunk(L, i, s, True)
                for s in range(2):
                    chunk(L, PAIRS - 1, s, False)

            act.wait_ge(flags_ready, 1)
            act.wait_ge(key_out, 16)
            chunks(0)
            for s in range(2):
                load_idx(1, 0, s)
                rebase_key(1, 0, s)

            def copy_transposed(g):
                act.wait_ge(hT_mm, g + 1)
                if g > 1:
                    act.wait_ge(tab_mm, g - 1)
                a, b = NODES[g]
                n = -(-(b - a) // TBL)
                nc.scalar.copy(hT[g % 2][0:D, 0:(b - a) * P].rearrange("f (k e) -> f k e", k=n),
                               ps_hT[g % 2][0:D, 0:n, 0:min(b - a, TBL) * P]).then_inc(hT_copied, 1)

            def copy_tables(g):
                act.wait_ge(tab_mm, g + 1)
                a, b = NODES[g]
                n = min(b - a, TBL)
                for z, tile in enumerate((cen, hid)):
                    last_copy = nc.scalar.copy(
                        tile[:, a:b, :].rearrange("p (k a) f -> p k a f", a=n),
                        ps_tab[g % 2][:, 0:(b - a) // n, 0:n * 2 * D].rearrange("p k (a c f) -> p k a c f", a=n, c=2)[:, :, :, z, :])
                last_copy.then_inc(table_ready[1], 1)
                act.wait_ge(table_ready[1], g + 1)
                cast_part(1, g, 0, cen, a, b)

            act.wait_ge(hT_set, 4)
            def root_of(g):
                if g < len(NODES):
                    root(len(FIRST) + g + 1, *NODES[g])

            root_of(0)
            copy_transposed(0)
            root_of(1)
            copy_tables(0)
            root_of(2)
            copy_transposed(1)
            root_of(3)
            for g in range(1, len(NODES)):
                if g + 1 < len(NODES):
                    copy_transposed(g + 1)
                copy_tables(g)
                root_of(g + 3)
            for n in range(1, SPLITS):
                for g, (a, b) in enumerate(NODES):
                    cast_part(1, g, n, cen, a, b)
            for s in range(2):
                act.wait_ge(stored[0][s], 16 * (PAIRS + 1 + s))
            act.wait_ge(keep_set, 1)
            chunks(1)

        @block.vector
        def _(dve):
            steps = [0]

            def step(ins):
                steps[0] += 1
                ins.then_inc(dve_step, 1)
                dve.wait_ge(dve_step, steps[0])

            def over_features(v, n=A):
                return v.unsqueeze(2).to_broadcast([P, n, D])

            def layernorm_relu(n, a, b):
                x_, c, h = xin[:, a:b, :], cen[:, a:b, :], hid[:, a:b, :]
                total, inverse, squares, std = (nstat[:, j, a:b] for j in range(4))
                step(nc.vector.tensor_reduce(total, x_, AX_X, ALU.add))
                step(nc.vector.scalar_tensor_tensor(c, over_features(total, b - a), -1.0 / D, x_, ALU.mult, ALU.add))
                step(nc.vector.tensor_tensor(h, c, c, ALU.mult))
                nc.vector.tensor_reduce(squares, h, AX_X, ALU.add).then_inc(squares_ready, 1)
                dve.wait_ge(std_ready, n)
                step(nc.vector.reciprocal(inverse, std))
                return nc.vector.scalar_tensor_tensor(h, c, 0.0, over_features(inverse, b - a), ALU.max, ALU.mult)

            def take_rest(L, g, n, tile, a, b):
                dve.wait_ge(part_cast[L][n], g + 1)
                v = pair_view(tile if n == 0 else atab, a, b)
                nc.vector.tensor_tensor(pair_view(atab, a, b), v, parts[:, a // 2:-(-b // 2), n, :], ALU.subtract
                                        ).then_inc(rest_ready[L][n], 1)

            nc.vector.memset(src_i[:, LAST:COLS], 0)
            nc.vector.memset(dst_i[:, LAST:COLS], N)
            nc.vector.memset(ln_eps[:], LN_EPS)
            nc.vector.memset(wcat[:], 0.0)
            nc.vector.memset(edge_i[:], -1)
            nc.vector.memset(xin[:, A - 1, :], 0.0).then_inc(pads_set, 1)
            nc.vector.memset(hid[:, A:A2, :], 0.0)
            dve.wait_ge(iota_done, 1)
            nc.vector.tensor_scalar(negj[:], pidx[:], -1.0, None, ALU.mult)
            nc.vector.tensor_copy(pidx_h[:], pidx[:])
            nc.vector.tensor_scalar(node[:], node[:], 0.5 - CENTRE, None, ALU.add).then_inc(consts_ready, 1)
            dve.wait_ge(cols_in, 16)
            cols_i = rows[0][:].rearrange("p t f -> p (t f)").bitcast(I32)[:, 0:COLS]
            low_i, high_i = (v[:].rearrange("p f t -> p (f t)").bitcast(I32)[:, 0:COLS] for v in state)
            keys = rows[1][:].rearrange("p t f -> p (t f)").bitcast(F16)[:, 0:COLS]
            nc.vector.tensor_scalar(low_i, cols_i, P - 1, None, ALU.bitwise_and)
            step(nc.vector.tensor_scalar(high_i, cols_i, 8, 7, ALU.logical_shift_right, ALU.logical_shift_left))
            nc.vector.tensor_tensor(keys, high_i, low_i, ALU.add).then_inc(keys_made, 1)
            for g, (a, b) in enumerate(FIRST):
                dve.wait_ge(x_in[g], 16 * (g + 1))
                layernorm_relu(g + 1, a, b).then_inc(table_ready[0], 1)
                if g == 0:
                    dve.wait_ge(edges_in, 64)
                    nc.vector.tensor_scalar(block_i, src_i[:], P, 7, ALU.bitwise_and, ALU.logical_shift_right
                                            ).then_inc(blocks_ready, 1)

            def onehot_of(L, s, h):
                return nc.vector.tensor_scalar(onehot[:, h, 0:Q[L][s] * P], key_view(L, s), float(h * P), None, ALU.is_equal)

            def onehots(L, k, s, first=0, end=NG):
                dve.wait_ge(key_ready[L], k + 1)
                for j, (a, b) in enumerate(GROUPS[first:end], first):
                    dve.wait_ge(groups_done[L], NG * k + j + 1)
                    for h in range(a, b):
                        last_one = onehot_of(L, s, h)
                    last_one.then_inc(onehot_ready[L], 1)

            dve.sem_inc(psum_read[0], 2)
            dve.sem_inc(psum_read[1], 2)
            dve.wait_ge(key_ready[0], 1)
            for j, (a, b) in enumerate(GROUPS):
                for h in range(a, b):
                    last_one = onehot_of(0, 0, h)
                    if h % (SPLITS + 1) < SPLITS - 1 and h // (SPLITS + 1) < len(FIRST):
                        g = h // (SPLITS + 1)
                        take_rest(0, g, h % (SPLITS + 1), hid, *FIRST[g])
                last_one.then_inc(onehot_ready[0], 1)

            dve.wait_ge(small_in, 16 * 7)
            dve.wait_ge(numbers_done, 1)
            nc.vector.tensor_copy(last[:], dst_i[:, COLS - 1:COLS])
            step(nc.vector.tensor_copy(edge[:], edge_i[:]))
            step(nc.vector.tensor_scalar(rowsel[:], fixsel[:], edge[:, 1:2], None, ALU.is_ge))
            nc.vector.tensor_scalar(dst_c[:], dst_i[:], float(-CENTRE), None, ALU.add)
            nc.vector.scalar_tensor_tensor(rowsel[:], fixsel[:], last[:], rowsel[:], ALU.is_lt, ALU.mult).then_inc(rowsel_ready, 1)
            nc.vector.memset(same[:, 0:1], 0.0)
            nc.vector.tensor_tensor(same[:, 1:COLS], dst_i[:, 1:COLS], dst_i[:, 0:COLS - 1], ALU.is_equal).then_inc(flags_ready, 1)
            nc.vector.memset(state[1][:, :, T], 0.0)
            step(nc.vector.memset(keep[:, :, 0], 0.0))
            dve.wait_ge(masks_ready, 1)

            def constants():
                nc.vector.memset(carryT[:, 0:1], 0.0)
                nc.vector.memset(carry[:, D:D + 1], 1.0)
                nc.vector.tensor_scalar(ident[:], iota_f[:], pidx[:], None, ALU.is_equal)
                nc.vector.tensor_scalar(shift[:], iota_f[:], -1.0, pidx[:], ALU.add, ALU.is_equal)
                step(nc.vector.tensor_scalar(wrap[:], iota_f[:], float(P - 1), pidx[:], ALU.add, ALU.is_equal))

            def cut_segments():
                step(nc.vector.tensor_tensor(flag[:, 0:1], edge[:, 0:1], edge[:, 1:2], ALU.is_equal))
                step(nc.vector.tensor_tensor(flag[:, 1:2], edge[:, 0:1], edge[:, 2:3], ALU.is_equal))
                step(nc.vector.tensor_tensor(flag[:, 2:3], edge[:, 0:1], edge[:, 3:4], ALU.is_equal))
                step(nc.vector.tensor_tensor(flag[:, 3:4], flag[:, 0:1], flag[:, 1:2], ALU.mult))
                step(nc.vector.tensor_tensor(flag[:, 4:5], flag[:, 3:4], flag[:, 2:3], ALU.mult))
                step(nc.vector.tensor_tensor(flag[:, 5:6], flag[:, 0:1], flag[:, 4:5], ALU.subtract))
                step(nc.vector.tensor_scalar(flag[:, 6:7], edge[:, 0:1], 1.0, None, ALU.add))
                step(nc.vector.tensor_tensor(flag[:, 6:7], flag[:, 6:7], flag[:, 5:6], ALU.mult))
                step(nc.vector.tensor_scalar(flag[:, 6:7], flag[:, 6:7], -1.0, None, ALU.add))
                step(nc.vector.tensor_scalar(fixsel[:], fixsel[:], flag[:, 6:7], None, ALU.is_equal))
                step(nc.vector.tensor_copy(through[0][:], flag[:, 3:4].to_broadcast([P, D])))
                step(nc.vector.tensor_scalar(through[1][:], through[0][:], BIG, -BIG, ALU.mult, ALU.add))

            def scan_chunk(L, i, s):
                k = 2 * i + s
                dve.wait_ge(msg_ready[L], k + 1)
                nc.vector.tensor_copy(msg[:, :, 0], state[1 - s][:, :, T]).then_inc(carried[L], 1)
                dve.wait_ge(carried[L], k + 1)
                ops = (ALU.mult, ALU.add) if L == 0 else (ALU.add, ALU.max)
                flat = [v[:].rearrange("p f t -> p (f t)") for v in (state[s], keep, msg)]
                nc.vector.tensor_tensor_scan(flat[0], flat[1], flat[2], 0.0, *ops).then_inc(scanned[L], 1)
                dve.wait_ge(scanned[L], k + 1)

            def pick(L, i, s, q):
                k = 2 * i + s
                dve.wait_ge(groups_done[L], NG * (k + 2))
                m = mask[:, bass.ds(k * T + G[L][s], q), :].rearrange("p q z -> p (q z)")
                for a, b in ((0, q // BANK), (q // BANK, -(-q // BANK))):
                    if a < b:
                        n = min(q - a * BANK, (b - a) * BANK)
                        c = n // (b - a) * 2
                        ins = nc.vector.tensor_tensor(
                            picked[:, a * BANK:a * BANK + n, :, :].rearrange("p (g q) z f -> p g (q z) f", g=b - a),
                            ps_gat[s][:, a:b, 0:c * D].rearrange("p g (c f) -> p g c f", f=D),
                            m[:, 2 * a * BANK:2 * (a * BANK + n)].rearrange("p (g c) -> p g c", c=c)
                            .unsqueeze(3).to_broadcast([P, b - a, c, D]), ALU.mult)
                ins.then_inc(psum_read[L], 1)
                dve.wait_ge(psum_read[L], k + 3)

            def sum_chunk(L, i, s, attr_dmas, extra=0):
                k = 2 * i + s
                q = Q[L][s] - extra
                own = attr[s][:, G[L][s]:T - extra, :]
                if L == 0:
                    dve.wait_ge(attr_in[s], 16 * (i + attr_dmas))
                    dve.wait_ge(gathered[0][s], 16 * (G[L][s] * (i + 1) + extra))
                    if extra:
                        theirs = attr[s][:, T - extra:T, :]
                        nc.vector.tensor_tensor(theirs, theirs, gat[s][:, G[L][s]:G[L][s] + extra, :], ALU.add)
                    theirs = attr[s][:, 0:G[L][s], :]
                    nc.vector.tensor_tensor(theirs, theirs, gat[s][:, 0:G[L][s], :], ALU.add).then_inc(half_summed, 1)
                    pick(L, i, s, q)
                    nc.vector.tensor_tensor(own, own, picked[:, 0:q, 0, :], ALU.add).then_inc(half_summed, 1)
                    dve.wait_ge(half_summed, 2 * (k + 1))
                    nc.vector.tensor_tensor(own, own, picked[:, 0:q, 1, :], ALU.add).then_inc(summed[L], 1)
                else:
                    pick(L, i, s, q)
                    nc.vector.tensor_tensor(own, picked[:, 0:q, 0, :], picked[:, 0:q, 1, :], ALU.add).then_inc(summed[L], 1)

            def layer(L):
                with dve.Fori(0, PAIRS - 1) as i:
                    for s in range(2):
                        onehots(L, 2 * i + s + 1, 1 - s)
                        sum_chunk(L, i, s, 1)
                        scan_chunk(L, i, s)
                i = PAIRS - 1
                for s in range(2):
                    if s == 0:
                        onehots(L, 2 * i + 1, 1)
                    if L == 0:
                        (constants, cut_segments)[s]()
                    sum_chunk(L, i, s, 2 if 0 < LAST - (2 * FULL + s) * T < T else 1, EXTRA if L == 0 and s == 1 else 0)
                    scan_chunk(L, i, s)

            layer(0)

            dve.wait_ge(row_read, 2 * CHUNKS + 1)
            step(nc.vector.tensor_tensor(cum[:], signs[:, 0, 0:A], signs[:, 1, 0:A], ALU.add))
            step(nc.vector.tensor_scalar(cum[:], cum[:], 0.5, COLS / 2.0, ALU.mult, ALU.add))
            step(nc.vector.tensor_scalar(scratch[:], rowno[:, 0:A], float(COLS), None, ALU.mult))
            nc.vector.tensor_tensor(cum[:], cum[:], scratch[:], ALU.add).then_inc(cum_ready, 1)
            dve.wait_ge(cum_ready, 1)
            step(nc.vector.tensor_scalar(scratch[:], cum[:], -1.0, 0.0, ALU.add, ALU.max))
            nc.vector.tensor_copy(end_i[:], scratch[:]).then_inc(end_ready, 1)
            dve.wait_ge(cum_mm, 1)
            step(nc.vector.tensor_tensor(has[:], cum[:], ps_row[:, 0:A], ALU.subtract))
            step(nc.vector.tensor_scalar(has[:], has[:], 0.0, 1.0, ALU.max, ALU.min))

            def stitch(L):
                nc.vector.tensor_copy(trail[:], state[1][:, :, T]).then_inc(trail_ready, 1)
                dve.wait_ge(trail_mm, L + 1)
                nc.vector.tensor_copy(trailT[:], ps_small[0:D, 0:P])
                step(nc.vector.tensor_copy(throughT[L][:], ps_small[0:D, P:2 * P]))
                ops = (ALU.mult, ALU.add) if L == 0 else (ALU.add, ALU.max)
                nc.vector.tensor_tensor_scan(carryT[:, 1:P + 1], throughT[L][:], trailT[:], 0.0, *ops).then_inc(carryT_ready, 1)
                dve.wait_ge(carry_mm, L + 1)
                nc.vector.tensor_copy(carry[:, 0:D], ps_small[:, 0:D]).then_inc(carry_ready, 1)

            def fix(a, b):
                n = b - a
                o = a % PB * (D + 1)
                return ps_fix[:, a // PB, o:o + n * (D + 1)].rearrange("p (a f) -> p a f", a=n)

            stitch(0)
            nc.vector.memset(cen[:, A:A2, :], 0.0)
            onehots(1, 0, 0, end=NG - 1)
            step(nc.vector.tensor_scalar(eps_t[:], eps_t[:], 1.0, None, ALU.add))
            step(nc.vector.scalar_tensor_tensor(xin[:], hid[:, 0:A, :], eps_t[:], xin[:], ALU.mult, ALU.add))
            dve.wait_ge(w_in, 64)
            nc.vector.tensor_tensor(wcat[0:D, 0:D], wcat[0:D, 0:D], wcat[0:D, D:2 * D], ALU.subtract)
            for a in range(0, A, PB):
                b = min(a + PB, A)
                dve.wait_ge(fix_mm, a // PB + 1)
                step(nc.vector.tensor_tensor(xin[:, a:b, :], xin[:, a:b, :], fix(a, b)[:, :, 0:D], ALU.add))
            for g, (a, b) in enumerate(NODES):
                dve.wait_ge(ends_in[0][g], 16 * (b - a))
                v = val[:, a:b, :]
                step(nc.vector.tensor_tensor(v, v, over_features(has[:, a:b], b - a), ALU.mult))
                step(nc.vector.tensor_tensor(xin[:, a:b, :], xin[:, a:b, :], v, ALU.add))
                layernorm_relu(g + 3, a, b).then_inc(hid_ready, 1)
            for n in range(SPLITS - 1):
                for g, (a, b) in enumerate(NODES):
                    take_rest(1, g, n, cen, a, b)
            onehots(1, 0, 0, first=NG - 1)
            nc.vector.memset(keep[:, :, 0], -BIG)
            nc.vector.memset(state[1][:, :, T], 0.0).then_inc(keep_set, 1)
            layer(1)

            stitch(1)
            dve.wait_ge(fix_mm, 2 * -(-A // PB))
            for g, (a, b) in enumerate(NODES):
                n = b - a
                c, f, ps = cen[:, a:b, :], fixpen[:, a:b], fix(a, b)
                step(nc.vector.tensor_scalar(f, ps[:, :, D], BIG, -BIG, ALU.mult, ALU.add))
                step(nc.vector.tensor_tensor(c, ps[:, :, 0:D], f.unsqueeze(2).to_broadcast([P, n, D]), ALU.add))
            for g, (a, b) in enumerate(NODES):
                v, c = val[:, a:b, :], cen[:, a:b, :]
                dve.wait_ge(ends_in[1][g], 16 * (b - a))
                step(nc.vector.tensor_tensor(v, v, c, ALU.max))
                step(nc.vector.tensor_tensor(v, v, hid[:, a:b, :], ALU.add))
                step(nc.vector.tensor_tensor(v, v, over_features(has[:, a:b], b - a), ALU.mult))
                nc.vector.tensor_tensor(v, v, xin[:, a:b, :], ALU.add).then_inc(out_ready, 1)

        @block.tensor
        def _(pe):
            def find_row(k, half):
                pe.wait_ge(rowsel_ready, 1)
                pe.wait_ge(row_read, 2 * k + half + 1)
                sel, cols = rowsel[:, bass.ds(k * P, P)], slice(half * HALF, (half + 1) * HALF)
                if half == 0:
                    nc.tensor.matmul(ps_row[:, HALF:HALF + 1], sel, pidx_h[:], start=True, stop=True)
                nc.tensor.matmul(ps_row[:, 0:HALF], sel, dst_c[:, cols], start=True, stop=True).then_inc(row_mm, 1)

            for L in range(2):
                pe.sem_inc(groups_done[L], NG)

            def gather_chunk(L, i, s, extra=0):
                k = 2 * i + s
                count = Q[L][s] - extra
                for j, (a, b) in enumerate(GROUPS):
                    pe.wait_ge(onehot_ready[L], NG * k + j + 1)
                    if j == 0:
                        pe.wait_ge(psum_read[L], k + 1)
                    if L == 0 and j == WITH_SECOND:
                        pe.wait_ge(part_cast[0][SPLITS - 1], len(FIRST))
                    for h in range(a, b):
                        w = D * min(A - 2 * h, 2)
                        for q in range(count):
                            for n in range(SPLITS):
                                o = q % BANK * 2 * D
                                last_one = nc.tensor.matmul(
                                    ps_gat[s][:, q // BANK, o:o + w], onehot[:, h, q * P:(q + 1) * P], parts[:, h, n, 0:w],
                                    start=(h == 0 and q % BANK == 0 and n == 0),
                                    stop=(h == H - 1 and n == SPLITS - 1 and (q % BANK == BANK - 1 or q == count - 1)))
                    last_one.then_inc(groups_done[L], 1)
                    if L == 0 and j >= NG - 2:
                        find_row(k, j - (NG - 2))

            def layer(L):
                for n in range(SPLITS):
                    pe.wait_ge(part_cast[L][n], (1, len(NODES))[L])
                with pe.Fori(0, PAIRS - 1) as i:
                    for s in range(2):
                        gather_chunk(L, i, s)
                gather_chunk(L, PAIRS - 1, 0)
                gather_chunk(L, PAIRS - 1, 1, (EXTRA, 0)[L])

            def stitch(L):
                pe.wait_ge(trail_ready, L + 1)
                nc.tensor.transpose(ps_small[0:D, 0:P], trail[:], ident[:])
                nc.tensor.transpose(ps_small[0:D, P:2 * P], through[L][:], ident[:]).then_inc(trail_mm, 1)
                pe.wait_ge(carryT_ready, L + 1)
                nc.tensor.transpose(ps_small[:, 0:D], carryT[:, 0:P], ident[0:D, 0:D]).then_inc(carry_mm, 1)
                pe.wait_ge(carry_ready, L + 1)
                for a in range(A):
                    o = (a % PB) * (D + 1)
                    last_one = nc.tensor.matmul(ps_fix[:, a // PB, o:o + D + 1], fixsel[:, a * P:(a + 1) * P], carry[:],
                                                start=True, stop=True)
                    if (a + 1) % PB == 0 or a == A - 1:
                        last_one.then_inc(fix_mm, 1)

            layer(0)
            pe.wait_ge(cum_ready, 1)
            nc.tensor.matmul(ps_row[:, 0:A], shift[:], cum[:], start=True, stop=False)
            nc.tensor.matmul(ps_row[:, 1:A], wrap[:], cum[:, 0:A - 1], start=False, stop=True).then_inc(cum_mm, 1)
            stitch(0)

            def transpose_hid(g):
                a, b = NODES[g]
                pe.wait_ge(hid_ready, g + 1)
                if g > 1:
                    pe.wait_ge(hT_copied, g - 1)
                for n in range(b - a):
                    last_one = nc.tensor.transpose(ps_hT[g % 2][0:D, n // TBL, n % TBL * P:(n % TBL + 1) * P],
                                                   hid[:, a + n, :], ident[:])
                last_one.then_inc(hT_mm, 1)

            def multiply_weights(g):
                a, b = NODES[g]
                pe.wait_ge(hT_copied, g + 1)
                if g > 1:
                    pe.wait_ge(table_ready[1], g - 1)
                for n in range(b - a):
                    o = n % TBL * 2 * D
                    last_one = nc.tensor.matmul(ps_tab[g % 2][:, n // TBL, o:o + 2 * D], hT[g % 2][:, n * P:(n + 1) * P], wcat[:],
                                                start=True, stop=True)
                last_one.then_inc(tab_mm, 1)

            transpose_hid(0)
            multiply_weights(0)
            transpose_hid(1)
            for g in range(1, len(NODES)):
                if g + 1 < len(NODES):
                    transpose_hid(g + 1)
                multiply_weights(g)
            layer(1)
            stitch(1)


def kernel(x, src, dst, edge_attr_48, L0_gnn_eps, L1_gnn_theta_w, L1_gnn_theta_b, L1_gnn_phi_w, L1_gnn_phi_b):
    import numpy as _np
    import concourse.bacc as _bacc
    from concourse import mybir as _mybir
    from concourse.bass_utils import run_bass_kernel_spmd as _run

    src = _np.asarray(src)
    runs = _np.zeros((P, -(-src.shape[0] // P)), src.dtype)
    runs.reshape(-1)[: src.shape[0]] = src
    ins = {
        "x": x, "src": src, "src_cols": runs.T, "dst": dst, "edge_attr": edge_attr_48, "eps": L0_gnn_eps,
        "theta_t": _np.asarray(L1_gnn_theta_w).T, "theta_b": L1_gnn_theta_b,
        "phi_t": _np.asarray(L1_gnn_phi_w).T, "phi_b": L1_gnn_phi_b,
    }
    nc = _bacc.Bacc("TRN2", target_bir_lowering=False, num_devices=1)
    arrays, args = {}, []
    for name, a in ins.items():
        a = _np.ascontiguousarray(a)
        arrays[f"in_{name}_dram"] = a
        args.append(nc.dram_tensor(f"in_{name}_dram", a.shape, _mybir.dt.from_np(a.dtype), kind="ExternalInput").ap())
    out = nc.dram_tensor("out_dram", tuple(_np.shape(x)), F32, kind="ExternalOutput").ap()
    gnn_two_layer_kernel(nc, *args, out)
    r = _run(nc, [arrays], core_ids=[0])
    return r.results[0]["out_dram"]
```
